# Optimizing a Trainium2 kernel written in Bass

```python
import numpy as np
import jax
import jax.numpy as jnp

def _softmax(x, axis=-1):
    return jax.nn.softmax(x, axis=axis)

def _gelu(x):
    return jax.nn.gelu(x, approximate=True)

def _silu(x):
    return jax.nn.silu(x)

def _sigmoid(x):
    return jax.nn.sigmoid(x)

def _layernorm(x, axis=-1, eps=1e-05):
    m = jnp.mean(x, axis=axis, keepdims=True)
    v = jnp.var(x, axis=axis, keepdims=True)
    return (x - m) / jnp.sqrt(v + eps)

def _scatter_add(tgt, idx, src, axis=0):
    return tgt.at[idx].add(src)

def _segment_sum(src, seg, n):
    return jax.ops.segment_sum(src, seg, n)
kernel_name = 'mk_flamingo_gated_d2_seqx_r4_faccf4'

def setup_inputs(seed: int=0):
    np.random.seed(seed)
    _w = jnp.asarray

    def _rec_inputs():
        import jax
        import jax.numpy as jnp
        _rk = jax.random.key(seed)
        x = 7.22e-05 + 1 * jax.random.normal(jax.random.fold_in(_rk, 1), (16, 128, 256), jnp.float32)
        _lenS = 128 - jax.random.randint(jax.random.fold_in(_rk, 7), (16,), 0, max(1, 128 // 4) + 1, jnp.int32)
        _lenS2 = 128 - jax.random.randint(jax.random.fold_in(_rk, 8), (16,), 0, max(1, 128 // 4) + 1, jnp.int32)
        _ctx_1024P = jax.random.normal(jax.random.fold_in(_rk, 11), (16, 16, 256), jnp.float32)
        _ctx_1024c = jax.random.dirichlet(jax.random.fold_in(_rk, 511), 0.3 * jnp.ones((16,), jnp.float32), (16, 128))
        _ctx_1024t = jnp.einsum('bsk,bkd->bsd', _ctx_1024c, _ctx_1024P)
        _ctx_1024t = _ctx_1024t * jax.lax.rsqrt(jnp.mean(jnp.square(_ctx_1024t)) + 1e-12) * 0.953939
        ctx_1024 = 4.13588e-05 + 0.999923 * (_ctx_1024t + 0.3 * jax.random.normal(jax.random.fold_in(_rk, 611), (16, 128, 256), jnp.float32))
        _validS = jnp.arange(128)[None, :] < _lenS[:, None]
        _validS2 = jnp.arange(128)[None, :] < _lenS2[:, None]
        _causal = jnp.tril(jnp.ones((128, 128), dtype=bool))
        mask_Bx1xSxS2_bf1 = jnp.ones((16, 1, 128, 128), dtype=bool)
        _g = jax.random.normal(jax.random.fold_in(_rk, 9001), (2, 2), jnp.float32)
        _g = jnp.sign(_g) * jnp.maximum(jnp.abs(_g), 1.0) + (_g == 0) * 1.0
        g_xattn = _g[0]
        g_ffn = _g[1]
        return (x, ctx_1024, mask_Bx1xSxS2_bf1, g_xattn, g_ffn)
    x, ctx_1024, mask_Bx1xSxS2_bf1, g_xattn, g_ffn = _rec_inputs()

    def _L0_xattn_setup():
        import jax, jax.numpy as jnp
        import numpy as np
        B, S, D, H, W = (2, 1024, 256, 16, 16)
        HD = D // H
        key = jax.random.key(seed)
        ks = jax.random.split(key, 10)
        std = 0.02
        mk_w = lambda k: jax.random.normal(k, (D, D), jnp.float32) * std
        mk_b = lambda k: jax.random.normal(k, (D,), jnp.float32) * std
        return {'query': jax.random.normal(ks[0], (B, S, D), jnp.float32), 'kv': jax.random.normal(ks[1], (B, S, D), jnp.float32), 'Wq': mk_w(ks[2]), 'bq': mk_b(ks[3]), 'Wk': mk_w(ks[4]), 'bk': mk_b(ks[5]), 'Wv': mk_w(ks[6]), 'bv': mk_b(ks[7]), 'Wo': mk_w(ks[8]), 'bo': mk_b(ks[9]), 'is_causal': 1}
    _L0_xattn_all = _L0_xattn_setup()
    _L0_xattn_in = {k: v for k, v in _L0_xattn_all.items() if k in ('Wq', 'bq', 'Wk', 'bk', 'Wv', 'bv', 'Wo', 'bo')}
    del _L0_xattn_all

    def _L0_ffn_setup():
        import jax, jax.numpy as jnp
        import numpy as np
        E = 8
        K = 2
        key = jax.random.key(seed)
        ks = jax.random.split(key, 8)
        B, T, d = (4, 512, 256)
        h = 4 * d // E
        s = 0.02
        X = jax.random.normal(ks[0], (B, T, d), jnp.float32)
        routing_W = jax.random.normal(ks[1], (E, d), jnp.float32) * s
        expert_bias = jnp.zeros((E,), jnp.float32)
        sW1 = jax.random.normal(ks[2], (d, h), jnp.float32) * s
        sb1 = jnp.zeros((h,), jnp.float32)
        sW2 = jax.random.normal(ks[3], (h, d), jnp.float32) * s
        sb2 = jnp.zeros((d,), jnp.float32)
        rW1 = jax.random.normal(ks[4], (E, d, h), jnp.float32) * s
        rb1 = jnp.zeros((E, h), jnp.float32)
        rW2 = jax.random.normal(ks[5], (E, h, d), jnp.float32) * s
        rb2 = jnp.zeros((E, d), jnp.float32)
        return dict(X=X, routing_W=routing_W, expert_bias=expert_bias, sW1=sW1, sb1=sb1, sW2=sW2, sb2=sb2, rW1=rW1, rb1=rb1, rW2=rW2, rb2=rb2)
    _L0_ffn_all = _L0_ffn_setup()
    _L0_ffn_in = {k: v for k, v in _L0_ffn_all.items() if k in ('routing_W', 'expert_bias', 'sW1', 'sb1', 'sW2', 'sb2', 'rW1', 'rb1', 'rW2', 'rb2')}
    del _L0_ffn_all

    def _L1_xattn_setup():
        import jax, jax.numpy as jnp
        import numpy as np
        D_MODEL = 256
        H = 16
        D_K = D_MODEL // H
        MAX_SEQ_LEN = 512
        B = 2
        S = 512
        key = jax.random.key(seed)
        ks = jax.random.split(key, 8)
        scale = 1.0 / np.sqrt(D_MODEL)
        return {'q': jax.random.normal(ks[0], (B, S, D_MODEL), jnp.float32), 'k': jax.random.normal(ks[1], (B, S, D_MODEL), jnp.float32), 'v': jax.random.normal(ks[2], (B, S, D_MODEL), jnp.float32), 'mask': jnp.ones((B, 1, S, S), dtype=bool), 'w_q': jax.random.normal(ks[3], (D_MODEL, D_MODEL), jnp.float32) * scale, 'w_k': jax.random.normal(ks[4], (D_MODEL, D_MODEL), jnp.float32) * scale, 'w_v': jax.random.normal(ks[5], (D_MODEL, D_MODEL), jnp.float32) * scale, 'w_o': jax.random.normal(ks[6], (D_MODEL, D_MODEL), jnp.float32) * scale, 'rel_emb': jax.random.normal(ks[7], (2 * MAX_SEQ_LEN - 1, H), jnp.float32) * 0.02}
    _L1_xattn_all = _L1_xattn_setup()
    _L1_xattn_in = {k: v for k, v in _L1_xattn_all.items() if k in ('w_q', 'w_k', 'w_v', 'w_o', 'rel_emb')}
    del _L1_xattn_all

    def _L1_ffn_setup():
        import jax, jax.numpy as jnp
        import numpy as np
        INT8_MAX = 127.0

        def _absmax_scale(x, axes):
            amax = jnp.max(jnp.abs(x), axis=axes, keepdims=True)
            return jnp.maximum(amax, 1e-12) / INT8_MAX
        key = jax.random.key(seed)
        k1, k2 = jax.random.split(key)
        lhs = jax.random.normal(k1, (4, 2048, 256), dtype=jnp.float32)
        rhs = jax.random.normal(k2, (256, 256), dtype=jnp.float32)
        return {'lhs': lhs, 'rhs': rhs}
    _L1_ffn_all = _L1_ffn_setup()
    _L1_ffn_in = {k: v for k, v in _L1_ffn_all.items() if k in ('rhs',)}
    del _L1_ffn_all
    return {'x': x, 'ctx_1024': ctx_1024, 'mask_Bx1xSxS2_bf1': mask_Bx1xSxS2_bf1, 'g_xattn': g_xattn, 'g_ffn': g_ffn, 'L0_xattn_Wq': _L0_xattn_in['Wq'], 'L0_xattn_bq': _L0_xattn_in['bq'], 'L0_xattn_Wk': _L0_xattn_in['Wk'], 'L0_xattn_bk': _L0_xattn_in['bk'], 'L0_xattn_Wv': _L0_xattn_in['Wv'], 'L0_xattn_bv': _L0_xattn_in['bv'], 'L0_xattn_Wo': _L0_xattn_in['Wo'], 'L0_xattn_bo': _L0_xattn_in['bo'], 'L0_ffn_routing_W': _L0_ffn_in['routing_W'], 'L0_ffn_expert_bias': _L0_ffn_in['expert_bias'], 'L0_ffn_sW1': _L0_ffn_in['sW1'], 'L0_ffn_sb1': _L0_ffn_in['sb1'], 'L0_ffn_sW2': _L0_ffn_in['sW2'], 'L0_ffn_sb2': _L0_ffn_in['sb2'], 'L0_ffn_rW1': _L0_ffn_in['rW1'], 'L0_ffn_rb1': _L0_ffn_in['rb1'], 'L0_ffn_rW2': _L0_ffn_in['rW2'], 'L0_ffn_rb2': _L0_ffn_in['rb2'], 'L1_xattn_w_q': _L1_xattn_in['w_q'], 'L1_xattn_w_k': _L1_xattn_in['w_k'], 'L1_xattn_w_v': _L1_xattn_in['w_v'], 'L1_xattn_w_o': _L1_xattn_in['w_o'], 'L1_xattn_rel_emb': _L1_xattn_in['rel_emb'], 'L1_ffn_rhs': _L1_ffn_in['rhs']}

def reference(x, ctx_1024, mask_Bx1xSxS2_bf1, g_xattn, g_ffn, L0_xattn_Wq, L0_xattn_bq, L0_xattn_Wk, L0_xattn_bk, L0_xattn_Wv, L0_xattn_bv, L0_xattn_Wo, L0_xattn_bo, L0_ffn_routing_W, L0_ffn_expert_bias, L0_ffn_sW1, L0_ffn_sb1, L0_ffn_sW2, L0_ffn_sb2, L0_ffn_rW1, L0_ffn_rb1, L0_ffn_rW2, L0_ffn_rb2, L1_xattn_w_q, L1_xattn_w_k, L1_xattn_w_v, L1_xattn_w_o, L1_xattn_rel_emb, L1_ffn_rhs):
    import jax
    import jax.numpy as jnp

    def _L0_xattn_ref(query, kv, Wq, bq, Wk, bk, Wv, bv, Wo, bo, is_causal):
        import jax, jax.numpy as jnp
        import numpy as np
        B, S, D, H, W = (2, 1024, 256, 16, 16)
        HD = D // H
        b, s, d = query.shape

        def split_heads(x):
            return x.reshape(b, s, H, HD).transpose(0, 2, 1, 3)
        Q = split_heads(query @ Wq.T + bq)
        K = split_heads(kv @ Wk.T + bk)
        V = split_heads(kv @ Wv.T + bv)
        pad = W - 1
        Kp = jnp.pad(K, ((0, 0), (0, 0), (pad, 0), (0, 0)))
        Vp = jnp.pad(V, ((0, 0), (0, 0), (pad, 0), (0, 0)))
        idx = jnp.arange(s)[:, None] + jnp.arange(W)[None, :]
        Kw = Kp[:, :, idx]
        Vw = Vp[:, :, idx]
        scores = jnp.einsum('bhsd,bhswd->bhsw', Q, Kw) / np.sqrt(HD).astype(np.float32)
        if is_causal:
            mask = jnp.arange(W)[None, :] <= jnp.arange(s)[:, None]
            scores = jnp.where(mask[None, None], scores, -jnp.inf)
        attn = jax.nn.softmax(scores, axis=-1)
        out = jnp.einsum('bhsw,bhswd->bhsd', attn, Vw)
        out = out.transpose(0, 2, 1, 3).reshape(b, s, d)
        return out @ Wo.T + bo

    def _L0_ffn_ref(X, routing_W, expert_bias, sW1, sb1, sW2, sb2, rW1, rb1, rW2, rb2):
        import jax, jax.numpy as jnp
        import numpy as np
        E = 8
        K = 2
        B, T, d = X.shape
        shared = jax.nn.silu(X @ sW1 + sb1) @ sW2 + sb2
        logits = jnp.einsum('btd,ed->bte', X, routing_W) + expert_bias
        activation = jnp.sqrt(jax.nn.softplus(logits))
        top_vals, top_idx = jax.lax.top_k(activation, K)
        combine = jnp.sum(jax.nn.one_hot(top_idx, E, dtype=X.dtype) * top_vals[..., None], axis=-2)
        Xf = X.reshape(-1, d)
        cf = combine.reshape(-1, E)
        hdn = jax.nn.silu(jnp.einsum('nd,edh->enh', Xf, rW1) + rb1[:, None, :])
        y = jnp.einsum('enh,ehd->end', hdn, rW2) + rb2[:, None, :]
        routed = jnp.einsum('ne,end->nd', cf, y).reshape(B, T, d)
        return shared + routed

    def _L1_xattn_ref(q, k, v, mask, w_q, w_k, w_v, w_o, rel_emb):
        import jax, jax.numpy as jnp
        import numpy as np
        D_MODEL = 256
        H = 16
        D_K = D_MODEL // H
        MAX_SEQ_LEN = 512
        B = 2
        S = 512
        batch, seq_len, _ = q.shape
        query = (q @ w_q.T).reshape(batch, seq_len, H, D_K).transpose(0, 2, 1, 3)
        key_ = (k @ w_k.T).reshape(batch, seq_len, H, D_K).transpose(0, 2, 1, 3)
        value = (v @ w_v.T).reshape(batch, seq_len, H, D_K).transpose(0, 2, 1, 3)
        scores = jnp.einsum('bhqd,bhkd->bhqk', query, key_) / jnp.sqrt(jnp.float32(D_K))
        rng = jnp.arange(seq_len)
        rel_pos = rng[:, None] - rng[None, :] + (MAX_SEQ_LEN - 1)
        rel_bias = rel_emb[rel_pos]
        scores = scores + rel_bias.transpose(2, 0, 1)[None]
        scores = jnp.where(mask, scores, -1000000000.0)
        attn = jax.nn.softmax(scores, axis=-1)
        x = jnp.einsum('bhqk,bhkd->bhqd', attn, value)
        x = x.transpose(0, 2, 1, 3).reshape(batch, seq_len, H * D_K)
        return x @ w_o.T

    def _L1_ffn_ref(lhs, rhs):
        import jax, jax.numpy as jnp
        import numpy as np
        INT8_MAX = 127.0

        def _absmax_scale(x, axes):
            amax = jnp.max(jnp.abs(x), axis=axes, keepdims=True)
            return jnp.maximum(amax, 1e-12) / INT8_MAX
        lhs_scale = _absmax_scale(lhs, (2,))
        rhs_scale = _absmax_scale(rhs, (0,))
        q_lhs = jnp.clip(jnp.round(lhs / lhs_scale), -INT8_MAX, INT8_MAX).astype(jnp.int8)
        q_rhs = jnp.clip(jnp.round(rhs / rhs_scale), -INT8_MAX, INT8_MAX).astype(jnp.int8)
        acc = jax.lax.dot_general(q_lhs, q_rhs, (((2,), (0,)), ((), ())), preferred_element_type=jnp.int32)
        return acc.astype(jnp.float32) * lhs_scale * rhs_scale
    x = x + jnp.tanh(g_xattn[0]) * _L0_xattn_ref(_layernorm(x, axis=-1), ctx_1024, L0_xattn_Wq, L0_xattn_bq, L0_xattn_Wk, L0_xattn_bk, L0_xattn_Wv, L0_xattn_bv, L0_xattn_Wo, L0_xattn_bo, 1)
    x = x + jnp.tanh(g_ffn[0]) * _L0_ffn_ref(_layernorm(x, axis=-1), L0_ffn_routing_W, L0_ffn_expert_bias, L0_ffn_sW1, L0_ffn_sb1, L0_ffn_sW2, L0_ffn_sb2, L0_ffn_rW1, L0_ffn_rb1, L0_ffn_rW2, L0_ffn_rb2)
    x = x + jnp.tanh(g_xattn[1]) * _L1_xattn_ref(_layernorm(x, axis=-1), ctx_1024, ctx_1024, mask_Bx1xSxS2_bf1, L1_xattn_w_q, L1_xattn_w_k, L1_xattn_w_v, L1_xattn_w_o, L1_xattn_rel_emb)
    x = x + jnp.tanh(g_ffn[1]) * _L1_ffn_ref(_layernorm(x, axis=-1), L1_ffn_rhs)
    return x

_drawn_inputs = setup_inputs


def setup_inputs(seed=0):
    import zlib

    import numpy as np

    out = dict(_drawn_inputs(seed))
    spreads = {'g_ffn': (-1.0, 0.2),
     'L0_ffn_expert_bias': (0.0, 0.1),
     'L0_ffn_sb1': (0.0, 0.65),
     'L0_ffn_sb2': (0.0, 0.1),
     'L0_ffn_rb1': (0.0, 0.546),
     'L0_ffn_rb2': (0.0, 0.1)}
    factors = {'L0_xattn_Wq': 8.0,
     'L0_xattn_bq': 40.269,
     'L0_xattn_Wk': 8.0,
     'L0_xattn_bk': 64.0,
     'L0_xattn_bv': 5.547,
     'L0_xattn_bo': 3.087,
     'L1_xattn_rel_emb': 26.748}
    for name, (base, spread) in spreads.items():
        noise = np.random.default_rng([zlib.crc32(name.encode()), seed]).standard_normal(out[name].shape)
        drawn = base * np.exp(spread * noise) if base else spread * noise
        out[name] = jnp.asarray(drawn.astype(out[name].dtype))
    for name, factor in factors.items():
        out[name] = (out[name] * factor).astype(out[name].dtype)
    return out
```

```python
from contextlib import ExitStack

import concourse.bass as bass
from concourse import mybir

P = 128
F32 = mybir.dt.float32
F32R = mybir.dt.float32r
BF16 = mybir.dt.bfloat16
U8 = mybir.dt.uint8
ALU = mybir.AluOpType
ACT = mybir.ActivationFunctionType
AX_X = mybir.AxisListType.X

B, S, D = 16, 128, 256
H = 16
HD = D // H
W = 16
KC = D // P
E = 8
HID = 128
EPS = 1e-5
SCALE = HD ** -0.5
MASKED = -float(2 ** 100)
HUGE = 3.0e38
ROUND = 1.5 * 2 ** 23
UH = 4
NU = H // UH
UW = UH * S

ATT_W = 4 * KC * D
NE = E + 1
W1_W = NE * KC * HID
W2_W = NE * D


def column_consts():
    at, n = {}, 0
    for name, w in (("bq", KC), ("bk", KC), ("b1", NE), ("rw", KC * E), ("even", 1), ("odd", 1),
                    ("ncap", 1), ("npad", 1), ("ident", P), ("band", S), ("minus", 6)):
        at[name] = slice(n, n + w)
        n += w
    return at, n


COL, NCOL = column_consts()


def row_consts():
    at, n = {}, 0
    for name, w in (("bv", D), ("bo", D), ("eb", E), ("g", 4)):
        at[name] = slice(n, n + w)
        n += w
    return at, n


ROW, NROW = row_consts()
WP = 8
PROLOGUE, STEPS = 4, B + 2


def build(nc, x, ctxT, mask, weights, cols, rows, b2, rel, rhsT, out):
    with ExitStack() as ctx:
        def sb(name, shape, dt=F32):
            return ctx.enter_context(nc.sbuf_tensor(name, shape, dt))

        def ps(name, shape=(P, 512), dt=F32):
            return ctx.enter_context(nc.psum_tensor(name, list(shape), dt))

        def sem(name):
            return ctx.enter_context(nc.semaphore(name))

        NW = 2 * ATT_W + W1_W + W2_W
        PIECE = NW // WP
        w_raw = [sb(f"w_raw{i}", [P, PIECE]) for i in range(2)]
        w_hi = sb("w_hi", [P, NW], F32R)
        w_lo = sb("w_lo", [P, NW], F32R)
        col = sb("col", [P, NCOL])
        row = sb("row", [P, NROW])
        b2_sb = sb("b2_sb", [NE, D])
        rel_sb = sb("rel_sb", [P, H, S])
        rw_hi = sb("rw_hi", [P, KC * E], F32R)
        rw_lo = sb("rw_lo", [P, KC * E], F32R)
        bqs = sb("bqs", [P, KC])
        gate = sb("gate", [P, 4])
        gbo = sb("gbo", [P, D])
        half = sb("half", [P, E])
        minus_half = sb("minus_half", [P, 1])
        ident_b = sb("ident_b", [P, P], BF16)
        rhs_raw = sb("rhs_raw", [P, KC, D])
        rhs_am = sb("rhs_am", [P, 4 * KC])
        rhs_qT = sb("rhs_qT", [P, KC, D])
        rhs_q = sb("rhs_q", [P, KC, D], BF16)
        rhs_sc = sb("rhs_sc", [P, D])
        ident = col[:, COL["ident"]]
        band = col[:, COL["band"]]

        def csl(name, i=0, n=1):
            a = COL[name].start + i
            return col[:, a:a + n]

        class Norm:
            def __init__(self, n, bank):
                self.stat = sb(f"{n}_stat", [P, 6])
                self.mv = sb(f"{n}_mv", [P, 2])
                self.ve = sb(f"{n}_ve", [P, 1])
                self.rstd = sb(f"{n}_rstd", [P, 1])
                self.xn = sb(f"{n}_xn", [P, D])
                self.hi = sb(f"{n}_hi", [P, KC, S], F32R)
                self.lo = sb(f"{n}_lo", [P, KC, S], F32R)
                self.bank = bank
                self.stat_ready = sem(f"{n}_stat_ready")
                self.mv_ready = sem(f"{n}_mv_ready")
                self.ve_ready = sem(f"{n}_ve_ready")
                self.rstd_ready = sem(f"{n}_rstd_ready")
                self.xn_ready = sem(f"{n}_xn_ready")
                self.xt_ready = sem(f"{n}_xt_ready")
                self.hi_ready = sem(f"{n}_hi_ready")
                self.lo_ready = sem(f"{n}_lo_ready")

        class Attention:
            def __init__(self, n, which):
                self.which = which
                self.X, self.Y, self.Z = ps(f"{n}_X"), ps(f"{n}_Y"), ps(f"{n}_Z")
                self.norm = Norm(n, self.Z)
                self.w = which * ATT_W
                self.ctx_raw = [sb(f"{n}_ctx_raw{i}", [P, KC, S]) for i in range(2)]
                self.ctx_hi = sb(f"{n}_ctx_hi", [P, KC, S], F32R)
                self.ctx_lo = sb(f"{n}_ctx_lo", [P, KC, S], F32R)
                self.q = sb(f"{n}_q", [P, KC, S])
                self.k = sb(f"{n}_k", [P, KC, 2, S])
                self.v = sb(f"{n}_v", [P, H, HD + 1])
                self.t = sb(f"{n}_t", [P, NU, UH, S])
                self.nm = sb(f"{n}_nm", [P, H])
                self.nmc = sb(f"{n}_nmc", [P, H]) if which == 0 else self.nm
                self.p = self.t
                self.pt = sb(f"{n}_pt", [P, NU, UH, S])
                self.e0a = sb(f"{n}_e0a", [P, H])
                self.e0 = sb(f"{n}_e0", [P, H])
                self.den = sb(f"{n}_den", [P, H])
                self.rden = sb(f"{n}_rden", [P, H])
                self.o = sb(f"{n}_o", [P, H, HD])
                self.o_hi = sb(f"{n}_o_hi", [P, KC, S], F32R)
                self.o_lo = sb(f"{n}_o_lo", [P, KC, S], F32R)
                self.ctx_in = [sem(f"{n}_ctx_in{i}") for i in range(2)]
                for_each = ("ctx_hi_ready ctx_ready qk_ready v_ready q_done k_done v_done s_ready t_ready "
                            "nm_ready nmc_ready sub_done p_ready pt_ready pt_done av_ready e0a_ready e0_ready "
                            "den_ready rden_ready o_ready ot_ready o_hi_ready o_lo_ready y_ready x_done").split()
                (self.ctx_hi_ready, self.ctx_ready, self.qk_ready, self.v_ready, self.q_done, self.k_done,
                 self.v_done, self.s_ready, self.t_ready, self.nm_ready, self.nmc_ready, self.sub_done,
                 self.p_ready, self.pt_ready, self.pt_done, self.av_ready, self.e0a_ready, self.e0_ready,
                 self.den_ready, self.rden_ready, self.o_ready, self.ot_ready, self.o_hi_ready,
                 self.o_lo_ready, self.y_ready, self.x_done) = [sem(f"{n}_{k}") for k in for_each]
                if which == 0:
                    self.xb_ready = sem(f"{n}_xb_ready")

            def bank(self, u):
                return (self.X, self.Y)[u % 2]

        A0, A1 = Attention("a0", 0), Attention("a1", 1)

        x0 = [sb(f"x0_{i}", [P, D]) for i in range(2)]
        x0b = sb("x0b", [P, D])
        x1 = [sb(f"x1_{i}", [P, D]) for i in range(2)]
        x2 = [sb(f"x2_{i}", [P, D]) for i in range(2)]
        x3 = sb("x3", [P, D])
        y_sb = [sb(f"y_{i}", [P, D]) for i in range(2)]
        mask_u8 = [sb(f"mask_u8_{i}", [P, S], U8) for i in range(2)]
        mask_neg = sb("mask_neg", [P, S])
        bm = sb("bm", [P, H, S])

        F0, F1 = ps("F0"), ps("F1")
        FN = Norm("f", F0)
        lg, lab, lex, lln, lsp = (sb(n, [P, E]) for n in ("lg", "lab", "lex", "lln", "lsp"))
        act14 = sb("act14", [P, E + 6])
        mx8 = sb("mx8", [P, 8])
        rep8 = sb("rep8", [P, 8])
        zap = sb("zap", [P, E + 6])
        cf9 = sb("cf9", [P, NE])
        cfg = sb("cfg", [P, E])
        cfT = sb("cfT", [NE, S])
        h = sb("h", [P, NE, S])
        h_hi = sb("h_hi", [P, NE, S], F32R)
        h_lo = sb("h_lo", [P, NE, S], F32R)
        acc = [sb(f"acc_{i}", [P, D]) for i in range(2)]
        HU = [(0, 4), (4, 8), (8, 9)]
        (lgm_ready, lg_ready, lab_ready, lex_ready, lln_ready, lsp_ready, act_ready, mx_ready, rep_ready,
         zap_ready, cf_ready, cfg_ready, cft_ready, cft_done, hm_ready, h_ready, hh_ready, hl_ready, ym_ready,
         acc_ready) = [sem(n) for n in (
             "lgm_ready lg_ready lab_ready lex_ready lln_ready lsp_ready act_ready mx_ready rep_ready "
             "zap_ready cf_ready cfg_ready cft_ready cft_done hm_ready h_ready hh_ready hl_ready ym_ready "
             "acc_ready").split()]

        QN = Norm("q", None)
        am = sb("am", [P, 1])
        lsc = sb("lsc", [P, 1])
        rsc = sb("rsc", [P, 1])
        qf = sb("qf", [P, D])
        qc = sb("qc", [P, D])
        qb = sb("qb", [P, D], BF16)
        qT = sb("qT", [P, KC, S], BF16)
        qy = sb("qy", [P, D])
        (am_ready, lsc_ready, rsc_ready, qf_ready, qc_ready, qb_ready, qt_ready, qt_done, qm_ready, qy_ready,
         y_ready) = [sem(n) for n in (
             "am_ready lsc_ready rsc_ready qf_ready qc_ready qb_ready qt_ready qt_done qm_ready qy_ready "
             "y_ready").split()]

        x_in = [sem(f"x_in{i}") for i in range(2)]
        mask_in = [sem(f"mask_in{i}") for i in range(2)]
        y_out = [sem(f"y_out{i}") for i in range(2)]
        mneg_ready, bm_ready = sem("mneg_ready"), sem("bm_ready")
        w_in, c_in = [sem(f"w_in{i}") for i in range(2)], sem("c_in")
        w_high, w_split, gtanh = sem("w_high"), sem("w_split"), sem("gtanh")
        pool_set, act_set, dve_set = sem("pool_set"), sem("act_set"), sem("dve_set")
        r_t, r_q, r_s = sem("r_t"), sem("r_q"), sem("r_s")
        waits_apart = sem("waits_apart")


        def upto(eng, s, b, per=1, k=None):
            eng.wait_ge(s, b * per + (per if k is None else k))

        def before(eng, s, b, per=1, k=None):
            n = b * per + (per if k is None else k) - per
            if type(n) is not int or n > 0:
                eng.wait_ge(s, n)

        def before2(eng, s, b, per=1, k=None):
            n = b * per + (per if k is None else k) - 2 * per
            if type(n) is not int or n > 0:
                eng.wait_ge(s, n)

        def dma_nth(b, par):
            return (b - par) * 8 + 16

        def settled(eng):
            eng.wait_ge(pool_set, 7)
            eng.wait_ge(act_set, 1)
            eng.wait_ge(dve_set, 4)

        def apart(eng):
            eng.sem_inc(waits_apart, 1)

        def unit_heads(t, u):
            return t[:, :].rearrange("p (c u j) -> p c u j", c=KC, u=NU)[:, :, u, :]

        def run(eng, step):
            for s in range(PROLOGUE):
                step(s, s % 2)
            with eng.Fori(PROLOGUE // 2, B // 2, 1) as turn_:
                step(turn_ * 2, 0)
                step(turn_ * 2 + 1, 1)
            for s in range(B, STEPS):
                step(s, s % 2)

        def live(s, stage):
            return type(s) is not int or 0 <= s - stage < B

        def wslice(t, off, k, m0, m, width):
            a = off + k * width + m0
            return t[:, a:a + m]

        block = ctx.enter_context(nc.Block())

        @block.sync
        def _(sp):
            sp.dma_start(col[:, :], cols).then_inc(c_in, 16)
            sp.dma_start(row[:, :], rows.partition_broadcast(P)).then_inc(c_in, 16)
            sp.dma_start(b2_sb[:, :], b2).then_inc(c_in, 16)
            sp.dma_start(rhs_raw[:, :, :], rhsT).then_inc(c_in, 16)
            sp.dma_start(rel_sb[:, :, :], rel).then_inc(c_in, 16)
            for i in range(WP):
                if i >= 2:
                    sp.wait_ge(w_split, i - 1)
                sp.dma_start(w_raw[i % 2][:, :], weights[:, i * PIECE:(i + 1) * PIECE]).then_inc(w_in[i % 2], 16)

            def loads(s, par):
                if live(s, 0):
                    b = s
                    before2(sp, A0.xb_ready, b)
                    before2(sp, A0.norm.xn_ready, b)
                    apart(sp)
                    sp.dma_start(x0[par][:, :], x[b]).then_inc(x_in[par], 16)
                    before2(sp, A0.ctx_ready, b)
                    apart(sp)
                    sp.dma_start(A0.ctx_raw[par][:, :, :], ctxT[b]).then_inc(A0.ctx_in[par], 16)

            def loads2(s, par):
                if live(s, 1):
                    b = s - 1
                    par = 1 - par
                    before2(sp, A1.ctx_ready, b)
                    apart(sp)
                    sp.dma_start(A1.ctx_raw[par][:, :, :], ctxT[b]).then_inc(A1.ctx_in[par], 16)
                    before2(sp, mneg_ready, b)
                    apart(sp)
                    sp.dma_start(mask_u8[par][:, :], mask[b]).then_inc(mask_in[par], 16)

            def store(s, par):
                if live(s, 3):
                    b = s - 3
                    par = 1 - par
                    upto(sp, y_ready, b)
                    apart(sp)
                    sp.dma_start(out[b], y_sb[par][:, :]).then_inc(y_out[par], 16)

            def step(s, par):
                loads(s, par)
                loads2(s, par)
                store(s, par)

            run(sp, step)
            store(STEPS, STEPS % 2)
            for i in range(2):
                sp.wait_ge(y_out[i], 16 * (B // 2))

        @block.gpsimd
        def _(pool):
            g = nc.gpsimd
            pool.wait_ge(c_in, 80)
            g.memset(half[:, :], 0.5).then_inc(pool_set, 1)
            g.memset(minus_half[:, :], -0.5).then_inc(pool_set, 1)
            g.memset(A0.v[:, :, HD:HD + 1], 1.0).then_inc(pool_set, 1)
            g.memset(A1.v[:, :, HD:HD + 1], 1.0).then_inc(pool_set, 1)
            g.memset(rep8[:, :], -1.0).then_inc(pool_set, 1)
            g.memset(cf9[:, :], 1.0).then_inc(pool_set, 1)
            g.memset(act14[:, :], -1.0).then_inc(pool_set, 1)

            def ctx_split(A, b, par):
                before(pool, A.qk_ready, b)
                before(pool, A.v_ready, b)
                pool.wait_ge(A.ctx_in[par], dma_nth(b, par))
                apart(pool)
                g.tensor_copy(A.ctx_hi[:, :, :], A.ctx_raw[par][:, :, :]).then_inc(A.ctx_hi_ready, 1)
                upto(pool, A.ctx_hi_ready, b)
                g.tensor_tensor(A.ctx_lo[:, :, :], A.ctx_raw[par][:, :, :], A.ctx_hi[:, :, :].bitcast(F32),
                                ALU.subtract).then_inc(A.ctx_ready, 1)

            def rstd(N, b):
                upto(pool, N.mv_ready, b)
                apart(pool)
                g.tensor_scalar(N.ve[:, :], N.mv[:, 1:2], EPS, None, ALU.add).then_inc(N.ve_ready, 1)
                upto(pool, N.ve_ready, b)
                before(pool, N.xn_ready, b)
                g.tensor_tensor(N.rstd[:, :], N.ve[:, :], minus_half[:, :], ALU.pow).then_inc(N.rstd_ready, 1)

            def add_bo(b, par):
                pool.wait_ge(x_in[par], dma_nth(b, par))
                before(pool, A0.x_done, b)
                g.tensor_tensor(x0b[:, :], x0[par][:, :], gbo[:, :], ALU.add).then_inc(A0.xb_ready, 1)

            def bias_mask(b, par):
                pool.wait_ge(mask_in[par], dma_nth(b, par))
                before(pool, bm_ready, b, NU)
                apart(pool)
                g.tensor_scalar(mask_neg[:, :], mask_u8[par][:, :], 0.0, MASKED, ALU.is_equal,
                                ALU.mult).then_inc(mneg_ready, 1)
                upto(pool, mneg_ready, b)
                for u in range(NU):
                    before(pool, A1.t_ready, b, NU, u + 1)
                    g.tensor_tensor(bm[:, UH * u:UH * (u + 1), :], rel_sb[:, UH * u:UH * (u + 1), :],
                                    mask_neg[:, None, :].to_broadcast([P, UH, S]),
                                    ALU.add).then_inc(bm_ready, 1)

            def subtract(A, b, u):
                upto(pool, A.nmc_ready if A.which == 0 else A.nm_ready, b, NU, u + 1)
                t4 = A.t[:, u, :, :].rearrange("p (c j) t -> p c j t", c=KC)
                g.tensor_tensor(t4, t4, unit_heads(A.nmc, u)[:, :, :, None].to_broadcast([P, KC, 2, S]),
                                ALU.add).then_inc(A.sub_done, 1)

            def activation_root(b):
                upto(pool, lsp_ready, b)
                before(pool, cf_ready, b)
                g.tensor_tensor(act14[:, 0:E], lsp[:, :], half[:, :], ALU.pow).then_inc(act_ready, 1)

            def h_low(b):
                for i, (a, z) in enumerate(HU):
                    upto(pool, hh_ready, b, len(HU), i + 1)
                    before(pool, ym_ready, b, 5)
                    g.tensor_tensor(h_lo[:, a:z, :], h[:, a:z, :], h_hi[:, a:z, :].bitcast(F32),
                                    ALU.subtract).then_inc(hl_ready, 1)

            def step(s, par):
                s0, s1, s2 = live(s, 0), live(s, 1), live(s, 2)
                if s0:
                    ctx_split(A0, s, par)
                if s2:
                    ctx_split(A1, s - 2, par)
                    rstd(A1.norm, s - 2)
                    bias_mask(s - 2, par)
                if s0:
                    rstd(A0.norm, s)
                if s1:
                    rstd(FN, s - 1)
                if s0:
                    add_bo(s, par)
                if s1:
                    activation_root(s - 1)
                for u in range(NU):
                    if s0:
                        subtract(A0, s, u)
                    if s2:
                        subtract(A1, s - 2, u)
                if s1:
                    h_low(s - 1)
                if s2:
                    rstd(QN, s - 2)

            settled(pool)
            run(pool, step)

        @block.scalar
        def _(act):
            a = nc.scalar
            act.wait_ge(c_in, 80)
            a.activation(gate[:, :], row[:, ROW["g"]], ACT.Tanh).then_inc(gtanh, 1)
            a.activation(bqs[:, :], col[:, COL["bq"]], ACT.Copy, scale=SCALE).then_inc(act_set, 1)
            for i in range(WP):
                act.wait_ge(w_in[i % 2], 16 * (i // 2 + 1))
                a.activation(w_hi[:, i * PIECE:(i + 1) * PIECE], w_raw[i % 2][:, :], ACT.Copy).then_inc(w_high, 1)
            settled(act)

            def norm_hi(N, b, readers, per):
                upto(act, N.xt_ready, b)
                before(act, readers, b, per)
                a.activation(N.hi[:, :, :], N.bank[:, 0:D].rearrange("p (c t) -> p c t", c=KC),
                             ACT.Copy).then_inc(N.hi_ready, 1)

            def q_out(A, b):
                upto(act, A.qk_ready, b)
                before(act, A.s_ready, b, NU)
                if A.which == 0:
                    for c in range(KC):
                        i = a.activation(A.q[:, c, :], A.X[:, c * S:(c + 1) * S], ACT.Identity,
                                         bias=bqs[:, c:c + 1], scale=SCALE)
                    i.then_inc(A.q_done, 1)
                else:
                    a.activation(A.q[:, :, :], A.X[:, 0:D].rearrange("p (c t) -> p c t", c=KC), ACT.Copy,
                                 scale=SCALE).then_inc(A.q_done, 1)

            def v_out1(b):
                upto(act, A1.v_ready, b)
                before(act, A1.av_ready, b)
                a.activation(A1.v[:, :, 0:HD], A1.Y[:, 0:D].rearrange("p (h d) -> p h d", h=H),
                             ACT.Copy).then_inc(A1.v_done, 1)

            def exps(A, b, u):
                upto(act, A.sub_done, b, NU, u + 1)
                a.activation(A.p[:, u, :, :], A.t[:, u, :, :], ACT.Exp).then_inc(A.p_ready, 1)

            def pt_out(A, b, u):
                upto(act, A.pt_ready, b, NU, u + 1)
                before(act, A.av_ready, b)
                a.activation(A.pt[:, u, :, :], A.Z[:, :].rearrange("p (h t) -> p h t", h=UH),
                             ACT.Copy).then_inc(A.pt_done, 1)

            def pad_weight(b):
                upto(act, A0.e0a_ready, b)
                before(act, A0.den_ready, b)
                a.activation(A0.e0[:, :], A0.e0a[:, :], ACT.Exp).then_inc(A0.e0_ready, 1)

            def ot_hi(A, b):
                upto(act, A.ot_ready, b)
                before(act, A.y_ready, b)
                a.activation(A.o_hi[:, :, :], A.Y[:, 0:D].rearrange("p (c t) -> p c t", c=KC),
                             ACT.Copy).then_inc(A.o_hi_ready, 1)

            def softplus_log(b):
                upto(act, lab_ready, b)
                before(act, lln_ready, b)
                a.activation(lex[:, :], lab[:, :], ACT.Exp, scale=-1.0).then_inc(lex_ready, 1)
                upto(act, lex_ready, b)
                before(act, lsp_ready, b)
                a.activation(lln[:, :], lex[:, :], ACT.Ln, bias=1.0).then_inc(lln_ready, 1)

            def cft_out(b):
                upto(act, cft_ready, b)
                before(act, ym_ready, b, 5)
                a.activation(cfT[:, :], F1[0:NE, 0:S], ACT.Copy).then_inc(cft_done, 1)

            def silus(b, i):
                upto(act, hm_ready, b, len(HU), i + 1)
                before(act, hl_ready, b, len(HU), i + 1)
                before(act, hh_ready, b, len(HU), i + 1)
                lo, hi = HU[i]
                for e in range(lo, hi):
                    n = a.activation(h[:, e, :], (F0, F1)[i % 2][:, (e - lo) * S:(e - lo + 1) * S], ACT.Silu,
                                     bias=csl("b1", e))
                n.then_inc(h_ready, 1)

            def qt_out(b):
                upto(act, qt_ready, b)
                before(act, qm_ready, b)
                a.activation(qT[:, :, :], A1.Z[:, 0:D // 2].bitcast(BF16).rearrange("p (c t) -> p c t", c=KC),
                             ACT.Copy).then_inc(qt_done, 1)

            def step(s, par):
                s0, s1, s2 = live(s, 0), live(s, 1), live(s, 2)
                if s2:
                    norm_hi(A1.norm, s - 2, A1.qk_ready, 1)
                if s0:
                    norm_hi(A0.norm, s, A0.qk_ready, 1)
                if s1:
                    norm_hi(FN, s - 1, hm_ready, len(HU))
                if s2:
                    q_out(A1, s - 2)
                    v_out1(s - 2)
                if s0:
                    q_out(A0, s)
                if s1:
                    softplus_log(s - 1)
                for u in range(NU):
                    if s2:
                        exps(A1, s - 2, u)
                        pt_out(A1, s - 2, u)
                    if s0:
                        exps(A0, s, u)
                        pt_out(A0, s, u)
                if s0:
                    pad_weight(s)
                if s1:
                    cft_out(s - 1)
                if s2:
                    ot_hi(A1, s - 2)
                if s0:
                    ot_hi(A0, s)
                if s1:
                    for i in range(len(HU)):
                        silus(s - 1, i)
                if s2:
                    qt_out(s - 2)

            run(act, step)

        @block.vector
        def _(dve):
            v = nc.vector
            dve.wait_ge(c_in, 80)
            v.tensor_copy(ident_b[:, :], ident).then_inc(dve_set, 1)
            v.tensor_copy(rw_hi[:, :], col[:, COL["rw"]]).then_inc(dve_set, 1)
            dve.wait_ge(gtanh, 1)
            v.tensor_scalar(gbo[:, :], row[:, ROW["bo"]], gate[:, 0:1], None, ALU.mult).then_inc(dve_set, 1)
            for c in range(KC):
                i = v.tensor_reduce(rhs_am[:, c:c + 1], rhs_raw[:, c, :], AX_X, ALU.max, apply_absolute_value=True)
            i.then_inc(r_s, 1)
            dve.wait_ge(r_s, 1)
            v.tensor_scalar(rhs_am[:, 2:4], rhs_am[:, 0:2], 1e-12, 1.0 / 127.0, ALU.max, ALU.mult).then_inc(r_s, 1)
            dve.wait_ge(r_s, 2)
            v.reciprocal(rhs_am[:, 4:6], rhs_am[:, 2:4]).then_inc(r_s, 1)
            dve.wait_ge(r_s, 3)
            for c in range(KC):
                i = v.tensor_scalar(rhs_qT[:, c, :], rhs_raw[:, c, :], rhs_am[:, 4 + c:5 + c], ROUND,
                                    ALU.mult, ALU.add)
            i.then_inc(r_q, 1)
            dve.wait_ge(r_q, 1)
            v.tensor_scalar(rhs_qT[:, :, :], rhs_qT[:, :, :], ROUND + 127.0, ROUND - 127.0, ALU.min,
                            ALU.max).then_inc(r_q, 1)
            dve.wait_ge(r_q, 2)
            v.tensor_scalar(rhs_qT[:, :, :], rhs_qT[:, :, :], ROUND, None, ALU.subtract).then_inc(r_q, 1)
            dve.wait_ge(r_t, 1)
            v.tensor_copy(rhs_q[:, :, :], A0.X[:, :].rearrange("p (k n) -> p k n", k=KC)).then_inc(r_q, 1)
            v.tensor_copy(rhs_sc[:, :], A0.Y[:, 0:D]).then_inc(r_q, 1)
            for i in range(WP):
                dve.wait_ge(w_high, i + 1)
                v.tensor_tensor(w_lo[:, i * PIECE:(i + 1) * PIECE], w_raw[i % 2][:, :],
                                w_hi[:, i * PIECE:(i + 1) * PIECE].bitcast(F32), ALU.subtract).then_inc(w_split, 1)
            dve.wait_ge(dve_set, 2)
            v.tensor_tensor(rw_lo[:, :], col[:, COL["rw"]], rw_hi[:, :].bitcast(F32),
                            ALU.subtract).then_inc(dve_set, 1)
            settled(dve)

            def stats(N, b, src, wait):
                wait()
                v.bn_stats(N.stat[:, :], src).then_inc(N.stat_ready, 1)
                upto(dve, N.stat_ready, b)
                apart(dve)
                v.bn_aggr(N.mv[:, :], N.stat[:, :]).then_inc(N.mv_ready, 1)

            def normalise(N, b, src):
                upto(dve, N.rstd_ready, b)
                if N.bank is not None:
                    before(dve, N.xt_ready, b)
                v.tensor_scalar(N.xn[:, :], src, N.mv[:, 0:1], N.rstd[:, 0:1], ALU.subtract,
                                ALU.mult).then_inc(N.xn_ready, 1)

            def norm_lo(N, b, readers, per):
                upto(dve, N.hi_ready, b)
                before(dve, readers, b, per)
                v.tensor_tensor(N.lo[:, :, :], N.bank[:, 0:D].rearrange("p (c t) -> p c t", c=KC),
                                N.hi[:, :, :].bitcast(F32), ALU.subtract).then_inc(N.lo_ready, 1)

            def k_out(A, b):
                upto(dve, A.q_done, b)
                before(dve, A.s_ready, b, NU)
                for j, m in enumerate(("even", "odd")):
                    if A.which == 0:
                        for c in range(KC):
                            i = v.tensor_scalar(A.k[:, c, j, :], A.X[:, D + c * S:D + (c + 1) * S], csl("bk", c),
                                                csl(m), ALU.add, ALU.mult)
                    else:
                        i = v.tensor_scalar(A.k[:, :, j, :], A.X[:, D:2 * D].rearrange("p (c t) -> p c t", c=KC),
                                            csl(m), None, ALU.mult)
                i.then_inc(A.k_done, 1)

            def v_out0(b):
                upto(dve, A0.v_ready, b)
                before(dve, A0.av_ready, b)
                v.tensor_tensor(A0.v[:, :, 0:HD], A0.Y[:, 0:D].rearrange("p (h d) -> p h d", h=H),
                                row[:, ROW["bv"]].rearrange("p (h d) -> p h d", h=H),
                                ALU.add).then_inc(A0.v_done, 1)

            def maxima(A, b, u):
                upto(dve, A.s_ready, b, NU, u + 1)
                before(dve, A.pt_ready, b, NU, u + 1)
                if A.which == 0:
                    add = band[:, None, :].to_broadcast([P, UH, S])
                else:
                    upto(dve, bm_ready, b, NU, u + 1)
                    add = bm[:, UH * u:UH * (u + 1), :]
                v.tensor_tensor(A.t[:, u, :, :], A.bank(u)[:, :].rearrange("p (h t) -> p h t", h=UH), add,
                                ALU.add).then_inc(A.t_ready, 1)
                upto(dve, A.t_ready, b, NU, u + 1)
                before(dve, A.sub_done, b, NU, u + 1)
                v.tensor_reduce(unit_heads(A.nm, u), A.t[:, u, :, :].rearrange("p (c j) t -> p c j t", c=KC),
                                AX_X, ALU.max, negate=True).then_inc(A.nm_ready, 1)
                if A.which == 0:
                    upto(dve, A.nm_ready, b, NU, u + 1)
                    if u == 0:
                        before(dve, A.e0a_ready, b)
                    v.tensor_scalar(unit_heads(A.nmc, u), unit_heads(A.nm, u), csl("ncap"), None, ALU.min).then_inc(A.nmc_ready, 1)

            def pad_argument(b):
                upto(dve, A0.nmc_ready, b, NU)
                before(dve, A0.e0_ready, b)
                v.tensor_scalar(A0.e0a[:, :], A0.nmc[:, :], 0.0, None, ALU.min).then_inc(A0.e0a_ready, 1)

            def heads_out(A, b):
                upto(dve, A.av_ready, b)
                av = A.X[:, 0:H * (HD + 1)].rearrange("p (h d) -> p h d", h=H)
                if A.which == 0:
                    upto(dve, A.e0_ready, b)
                    before(dve, A.rden_ready, b)
                    v.scalar_tensor_tensor(out=A.den[:, :], in0=A.e0[:, :], scalar=csl("npad"), in1=av[:, :, HD],
                                           op0=ALU.mult, op1=ALU.add).then_inc(A.den_ready, 1)
                    upto(dve, A.den_ready, b)
                    before(dve, A.o_ready, b)
                    v.reciprocal(A.rden[:, :], A.den[:, :]).then_inc(A.rden_ready, 1)
                else:
                    before(dve, A.o_ready, b)
                    v.reciprocal(A.rden[:, :], av[:, :, HD]).then_inc(A.rden_ready, 1)
                upto(dve, A.rden_ready, b)
                before(dve, A.ot_ready, b)
                v.tensor_tensor(A.o[:, :, :], av[:, :, 0:HD], A.rden[:, :, None].to_broadcast([P, H, HD]),
                                ALU.mult).then_inc(A.o_ready, 1)

            def ot_lo(A, b):
                upto(dve, A.o_hi_ready, b)
                before(dve, A.y_ready, b)
                v.tensor_tensor(A.o_lo[:, :, :], A.Y[:, 0:D].rearrange("p (c t) -> p c t", c=KC),
                                A.o_hi[:, :, :].bitcast(F32), ALU.subtract).then_inc(A.o_lo_ready, 1)

            def residual0(b, par):
                upto(dve, A0.y_ready, b)
                upto(dve, A0.xb_ready, b)
                before2(dve, acc_ready, b, NE)
                v.scalar_tensor_tensor(out=x1[par][:, :], in0=A0.Z[:, 0:D], scalar=gate[:, 0:1], in1=x0b[:, :],
                                       op0=ALU.mult, op1=ALU.add).then_inc(A0.x_done, 1)

            def residual1(b, par):
                upto(dve, A1.y_ready, b)
                before(dve, y_ready, b)
                v.scalar_tensor_tensor(out=x3[:, :], in0=A1.Z[:, 0:D], scalar=gate[:, 1:2], in1=x2[par][:, :],
                                       op0=ALU.mult, op1=ALU.add).then_inc(A1.x_done, 1)

            def router(b):
                upto(dve, lgm_ready, b)
                before(dve, lsp_ready, b)
                v.tensor_tensor(lg[:, :], F1[:, 0:E], row[:, ROW["eb"]], ALU.add).then_inc(lg_ready, 1)
                upto(dve, lg_ready, b)
                before(dve, lex_ready, b)
                v.scalar_tensor_tensor(out=lab[:, :], in0=lg[:, :], scalar=-1.0, in1=lg[:, :], op0=ALU.mult,
                                       op1=ALU.max).then_inc(lab_ready, 1)

            def softplus(b):
                upto(dve, lln_ready, b)
                before(dve, act_ready, b)
                v.scalar_tensor_tensor(out=lsp[:, :], in0=lg[:, :], scalar=0.0, in1=lln[:, :], op0=ALU.max,
                                       op1=ALU.add).then_inc(lsp_ready, 1)

            def top_two(b):
                upto(dve, act_ready, b)
                before(dve, rep_ready, b)
                apart(dve)
                v.max(mx8[:, :], act14[:, 0:E]).then_inc(mx_ready, 1)
                upto(dve, mx_ready, b)
                before(dve, zap_ready, b)
                v.tensor_copy(rep8[:, 0:2], mx8[:, 0:2]).then_inc(rep_ready, 1)
                upto(dve, rep_ready, b)
                before(dve, cf_ready, b)
                apart(dve)
                v.match_replace(zap[:, :], rep8[:, :], act14[:, :], 0.0).then_inc(zap_ready, 1)
                upto(dve, zap_ready, b)
                before(dve, cft_ready, b)
                before(dve, cfg_ready, b)
                v.tensor_tensor(cf9[:, 0:E], act14[:, 0:E], zap[:, 0:E], ALU.subtract).then_inc(cf_ready, 1)
                upto(dve, cf_ready, b)
                before(dve, acc_ready, b, NE)
                v.tensor_scalar(cfg[:, :], cf9[:, 0:E], gate[:, 2:3], None, ALU.mult).then_inc(cfg_ready, 1)

            def h_high(b, i):
                lo, hi = HU[i]
                upto(dve, h_ready, b, len(HU), i + 1)
                before(dve, ym_ready, b, 5)
                v.tensor_copy(h_hi[:, lo:hi, :], h[:, lo:hi, :]).then_inc(hh_ready, 1)

            def combine(b, par):
                upto(dve, ym_ready, b, 5, 1)
                if True:
                    v.scalar_tensor_tensor(out=acc[0][:, :], in0=F1[:, 0:D], scalar=gate[:, 2:3],
                                           in1=x1[par][:, :], op0=ALU.mult, op1=ALU.add).then_inc(acc_ready, 1)
                upto(dve, cfg_ready, b)
                for e in range(E):
                    if e % 2 == 0:
                        upto(dve, ym_ready, b, 5, 2 + e // 2)
                    bank = (F0, F1)[(e // 2) % 2]
                    upto(dve, acc_ready, b, NE, e + 1)
                    if e == E - 1:
                        before2(dve, A1.x_done, b)
                    v.scalar_tensor_tensor(out=x2[par][:, :] if e == E - 1 else acc[(e + 1) % 2][:, :],
                                           in0=bank[:, (e % 2) * D:(e % 2 + 1) * D], scalar=cfg[:, e:e + 1],
                                           in1=acc[e % 2][:, :], op0=ALU.mult, op1=ALU.add).then_inc(acc_ready, 1)

            def quantise(b):
                upto(dve, QN.xn_ready, b)
                before(dve, lsc_ready, b)
                v.tensor_reduce(am[:, :], QN.xn[:, :], AX_X, ALU.max, apply_absolute_value=True).then_inc(am_ready, 1)
                upto(dve, am_ready, b)
                before(dve, qy_ready, b)
                v.tensor_scalar(lsc[:, :], am[:, :], 1e-12, 1.0 / 127.0, ALU.max, ALU.mult).then_inc(lsc_ready, 1)
                upto(dve, lsc_ready, b)
                v.reciprocal(rsc[:, :], lsc[:, :]).then_inc(rsc_ready, 1)
                upto(dve, rsc_ready, b)
                v.tensor_scalar(qf[:, :], QN.xn[:, :], rsc[:, 0:1], ROUND, ALU.mult, ALU.add).then_inc(qf_ready, 1)
                upto(dve, qf_ready, b)
                v.tensor_scalar(qc[:, :], qf[:, :], ROUND + 127.0, ROUND - 127.0, ALU.min,
                                ALU.max).then_inc(qc_ready, 1)
                upto(dve, qc_ready, b)
                before(dve, qt_ready, b)
                v.tensor_scalar(qb[:, :], qc[:, :], ROUND, None, ALU.subtract).then_inc(qb_ready, 1)

            def final(b, par):
                upto(dve, qm_ready, b)
                v.scalar_tensor_tensor(out=qy[:, :], in0=A1.X[:, 0:D], scalar=lsc[:, 0:1], in1=rhs_sc[:, :],
                                       op0=ALU.mult, op1=ALU.mult).then_inc(qy_ready, 1)
                upto(dve, qy_ready, b)
                n = dma_nth(b, par) - 16
                if type(n) is not int or n > 0:
                    dve.wait_ge(y_out[par], n)
                v.scalar_tensor_tensor(out=y_sb[par][:, :], in0=qy[:, :], scalar=gate[:, 3:4], in1=x3[:, :],
                                       op0=ALU.mult, op1=ALU.add).then_inc(y_ready, 1)

            def step(s, par):
                s0, s1, s2 = live(s, 0), live(s, 1), live(s, 2)
                b0, b1, b2 = s, s - 1, s - 2
                if s2:
                    stats(A1.norm, b2, x2[par][:, :], lambda: upto(dve, acc_ready, b2, NE))
                if s0:
                    stats(A0.norm, b0, x0[par][:, :], lambda: dve.wait_ge(x_in[par], dma_nth(b0, par)))
                if s1:
                    stats(FN, b1, x1[1 - par][:, :], lambda: upto(dve, A0.x_done, b1))
                if s2:
                    normalise(A1.norm, b2, x2[par][:, :])
                if s0:
                    normalise(A0.norm, b0, x0[par][:, :])
                if s1:
                    normalise(FN, b1, x1[1 - par][:, :])
                if s2:
                    norm_lo(A1.norm, b2, A1.qk_ready, 1)
                if s0:
                    norm_lo(A0.norm, b0, A0.qk_ready, 1)
                if s1:
                    norm_lo(FN, b1, hm_ready, len(HU))
                if s2:
                    k_out(A1, b2)
                if s0:
                    k_out(A0, b0)
                    v_out0(b0)
                if s1:
                    router(b1)
                for u in range(NU):
                    if s0:
                        maxima(A0, b0, u)
                    if s2:
                        maxima(A1, b2, u)
                    if s1 and u == 0:
                        softplus(b1)
                    if s1 and u == 1:
                        top_two(b1)
                if s0:
                    pad_argument(b0)
                if s2:
                    heads_out(A1, b2)
                if s0:
                    heads_out(A0, b0)
                if s2:
                    ot_lo(A1, b2)
                if s0:
                    ot_lo(A0, b0)
                if s2:
                    residual1(b2, par)
                    stats(QN, b2, x3[:, :], lambda: upto(dve, A1.x_done, b2))
                if s0:
                    residual0(b0, par)
                if s1:
                    for i in range(len(HU)):
                        h_high(b1, i)
                if s2:
                    normalise(QN, b2, x3[:, :])
                    quantise(b2)
                if s1:
                    combine(b1, 1 - par)
                if s2:
                    final(b2, par)

            run(dve, step)

        @block.tensor
        def _(pe):
            t = nc.tensor

            def split3(out_ap, l_hi, l_lo, r_hi, r_lo, first=True, last=True):
                t.matmul(out_ap, l_hi, r_hi, start=first, stop=False)
                t.matmul(out_ap, l_hi, r_lo, start=False, stop=False)
                return t.matmul(out_ap, l_lo, r_hi, start=False, stop=last)

            pe.wait_ge(c_in, 80)
            pe.wait_ge(r_q, 3)
            for k in range(KC):
                for n in range(KC):
                    t.transpose(A0.X[:, k * D + n * P:k * D + (n + 1) * P], rhs_qT[:, n, k * P:(k + 1) * P], ident)
            for n in range(KC):
                i = t.matmul(A0.Y[:, n * P:(n + 1) * P], rhs_am[:, 2 + n:3 + n].to_broadcast([P, P]), ident,
                             start=True, stop=True)
            i.then_inc(r_t, 1)
            pe.wait_ge(r_q, 5)
            pe.wait_ge(w_split, WP)
            settled(pe)

            def norm_t(N, b, free):
                upto(pe, N.xn_ready, b)
                free()
                for c in range(KC):
                    i = t.transpose(N.bank[:, c * S:(c + 1) * S], N.xn[:, c * P:(c + 1) * P], ident)
                i.then_inc(N.xt_ready, 1)

            def qk(A, b, free):
                upto(pe, A.norm.lo_ready, b)
                upto(pe, A.ctx_ready, b)
                free()
                for j, (hi, lo) in enumerate(((A.norm.hi, A.norm.lo), (A.ctx_hi, A.ctx_lo))):
                    off = A.w + j * KC * D
                    for c in range(KC):
                        o = A.X[:, j * D + c * S:j * D + (c + 1) * S]
                        for k in range(KC):
                            i = split3(o, wslice(w_hi, off, k, c * P, P, D), wslice(w_lo, off, k, c * P, P, D),
                                       hi[:, k, :], lo[:, k, :], k == 0, k == KC - 1)
                i.then_inc(A.qk_ready, 1)

            def vproj(A, b, free):
                free()
                off = A.w + 2 * KC * D
                for k in range(KC):
                    i = split3(A.Y[:, 0:D], A.ctx_hi[:, k, :], A.ctx_lo[:, k, :], wslice(w_hi, off, k, 0, D, D),
                               wslice(w_lo, off, k, 0, D, D), k == 0, k == KC - 1)
                i.then_inc(A.v_ready, 1)

            def scores(A, b, u):
                if u == 0:
                    upto(pe, A.k_done, b)
                if u == 1:
                    upto(pe, A.v_done, b)
                if u >= 2:
                    upto(pe, A.t_ready, b, NU, u - 1)
                for g in range(2):
                    r = 2 * HD * u
                    i = t.matmul(A.bank(u)[:, g * 2 * S:(g + 1) * 2 * S], A.q[r:r + 2 * HD, g, :],
                                 A.k[r:r + 2 * HD, g, :, :], start=True, stop=True)
                i.then_inc(A.s_ready, 1)

            def weights_t(A, b, u):
                upto(pe, A.p_ready, b, NU, u + 1)
                if u > 0:
                    upto(pe, A.pt_done, b, NU, u)
                for j in range(UH):
                    i = t.transpose(A.Z[:, j * S:(j + 1) * S], A.p[:, u, j, :], ident)
                i.then_inc(A.pt_ready, 1)

            def weighted(A, b):
                upto(pe, A.pt_done, b, NU)
                upto(pe, A.t_ready, b, NU, 3)
                for hh in range(H):
                    c, u, j = hh // (H // KC), hh // 2 % NU, hh % 2
                    i = t.matmul(A.X[:, hh * (HD + 1):(hh + 1) * (HD + 1)], A.pt[:, u, 2 * c + j, :],
                                 A.v[:, hh, :], start=True, stop=True)
                i.then_inc(A.av_ready, 1)

            def out_t(A, b):
                upto(pe, A.o_ready, b)
                o = A.o[:, :, :].rearrange("p h d -> p (h d)")
                for c in range(KC):
                    i = t.transpose(A.Y[:, c * S:(c + 1) * S], o[:, c * P:(c + 1) * P], ident)
                i.then_inc(A.ot_ready, 1)

            def out_proj(A, b):
                upto(pe, A.o_lo_ready, b)
                off = A.w + 3 * KC * D
                for k in range(KC):
                    i = split3(A.Z[:, 0:D], A.o_hi[:, k, :], A.o_lo[:, k, :], wslice(w_hi, off, k, 0, D, D),
                               wslice(w_lo, off, k, 0, D, D), k == 0, k == KC - 1)
                i.then_inc(A.y_ready, 1)

            def logits(b):
                upto(pe, FN.lo_ready, b)
                before(pe, acc_ready, b, NE)
                for k in range(KC):
                    i = split3(F1[:, 0:E], FN.hi[:, k, :], FN.lo[:, k, :], rw_hi[:, k * E:(k + 1) * E],
                               rw_lo[:, k * E:(k + 1) * E], k == 0, k == KC - 1)
                i.then_inc(lgm_ready, 1)

            def gates_t(b):
                upto(pe, cf_ready, b)
                upto(pe, lg_ready, b)
                t.transpose(F1[0:NE, 0:S], cf9[:, :], ident).then_inc(cft_ready, 1)

            def hidden(b, i):
                if i == 0:
                    upto(pe, FN.lo_ready, b)
                if i == 1:
                    upto(pe, cft_done, b)
                if i == 2:
                    upto(pe, h_ready, b, len(HU), 1)
                lo, hi = HU[i]
                for e in range(lo, hi):
                    o = (F0, F1)[i % 2][:, (e - lo) * S:(e - lo + 1) * S]
                    off = 2 * ATT_W + e * KC * HID
                    for k in range(KC):
                        n = split3(o, wslice(w_hi, off, k, 0, HID, HID), wslice(w_lo, off, k, 0, HID, HID),
                                   FN.hi[:, k, :], FN.lo[:, k, :], k == 0, k == KC - 1)
                n.then_inc(hm_ready, 1)

            def expert(bank, e, half_, first):
                off = 2 * ATT_W + W1_W + e * D
                return split3(bank[:, half_ * D:(half_ + 1) * D], h_hi[:, e, :], h_lo[:, e, :],
                              w_hi[:, off:off + D], w_lo[:, off:off + D], first, True)

            def shared_out(b):
                upto(pe, h_ready, b, len(HU), 2)
                upto(pe, hl_ready, b, len(HU), 1)
                t.matmul(F1[:, 0:D], cfT[:, :], b2_sb[:, :], start=True, stop=False)
                expert(F1, 0, 0, False).then_inc(ym_ready, 1)

            def pair_out(b, j):
                if j == 0:
                    upto(pe, h_ready, b, len(HU))
                    upto(pe, hl_ready, b, len(HU), 1)
                if j == 1:
                    upto(pe, hl_ready, b, len(HU), 2)
                    upto(pe, acc_ready, b, NE, 1)
                if j == 3:
                    upto(pe, hl_ready, b, len(HU), 3)
                if j >= 2:
                    upto(pe, acc_ready, b, NE, 2 * (j - 2) + 3)
                bank = (F0, F1)[j % 2]
                expert(bank, 1 + 2 * j, 0, True)
                expert(bank, 2 + 2 * j, 1, True).then_inc(ym_ready, 1)

            def q_t(b):
                upto(pe, qb_ready, b)
                for c in range(KC):
                    i = t.transpose(A1.Z[:, c * (S // 2):(c + 1) * (S // 2)].bitcast(BF16), qb[:, c * P:(c + 1) * P],
                                    ident_b[:, :])
                i.then_inc(qt_ready, 1)

            def q_mm(b):
                upto(pe, qt_done, b)
                for k in range(KC):
                    i = t.matmul(A1.X[:, 0:D], qT[:, k, :], rhs_q[:, k, :], start=(k == 0), stop=(k == KC - 1))
                i.then_inc(qm_ready, 1)

            def step(s, par):
                s0, s1, s2 = live(s, 0), live(s, 1), live(s, 2)
                b0, b1, b2 = s, s - 1, s - 2
                if s2:
                    norm_t(A1.norm, b2, lambda: before(pe, qt_done, b2))
                if s0:
                    norm_t(A0.norm, b0, lambda: before(pe, A0.x_done, b0))
                if s1:
                    norm_t(FN, b1, lambda: before(pe, acc_ready, b1, NE))
                if s2:
                    qk(A1, b2, lambda: before(pe, qy_ready, b2))
                    vproj(A1, b2, lambda: before(pe, A1.o_lo_ready, b2))
                if s0:
                    qk(A0, b0, lambda: before(pe, A0.o_ready, b0))
                    vproj(A0, b0, lambda: before(pe, A0.o_lo_ready, b0))
                if s1:
                    logits(b1)
                for u in range(2):
                    if s0:
                        scores(A0, b0, u)
                    if s2:
                        scores(A1, b2, u)
                if s1:
                    hidden(b1, 0)
                for u in range(NU):
                    if s2:
                        weights_t(A1, b2, u)
                    if s0:
                        weights_t(A0, b0, u)
                    if u + 2 < NU:
                        if s0:
                            scores(A0, b0, u + 2)
                        if s2:
                            scores(A1, b2, u + 2)
                if s2:
                    weighted(A1, b2)
                if s0:
                    weighted(A0, b0)
                if s1:
                    gates_t(b1)
                if s2:
                    out_t(A1, b2)
                if s0:
                    out_t(A0, b0)
                if s2:
                    out_proj(A1, b2)
                if s0:
                    out_proj(A0, b0)
                if s1:
                    hidden(b1, 1)
                    hidden(b1, 2)
                    shared_out(b1)
                    for j in range(E // 2):
                        if j == 1 and s2:
                            q_t(b2)
                        if j == 3 and s2:
                            q_mm(b2)
                        pair_out(b1, j)
                elif s2:
                    q_t(b2)
                    q_mm(b2)

            run(pe, step)


_INS = ("x", "ctxT", "mask", "weights", "cols", "rows", "b2", "rel", "rhsT")


def lay_out(i):
    import numpy as np

    def a(n):
        return np.ascontiguousarray(i[n])

    def chunks(w):
        return w.reshape(-1, P, w.shape[-1]).transpose(1, 0, 2).reshape(P, -1)

    att = [chunks(a(f"L{layer}_xattn_{n}").T) for layer, names in ((0, ("Wq", "Wk", "Wv", "Wo")),
                                                                  (1, ("w_q", "w_k", "w_v", "w_o"))) for n in names]
    w1 = [chunks(a("L0_ffn_sW1"))] + [chunks(w) for w in a("L0_ffn_rW1")]
    w2 = [a("L0_ffn_sW2")] + list(a("L0_ffn_rW2"))
    weights = np.concatenate(att + w1 + w2, axis=1)
    r = np.arange(P)
    f = np.float32
    q, key = r[:, None], r[None, :]
    inside = (key - q + W - 1 >= 0) & (key <= q) & (key - q + W - 1 <= q)
    pads = np.where(r < W - 1, np.minimum(r, W - 2 - r) + 1, 0)
    cols = np.concatenate([
        a("L0_xattn_bq").reshape(KC, P).T, a("L0_xattn_bk").reshape(KC, P).T,
        np.concatenate([a("L0_ffn_sb1")[None], a("L0_ffn_rb1")]).T,
        chunks(a("L0_ffn_routing_W").T),
        (r // HD % 2 == 0).astype(f)[:, None], (r // HD % 2 == 1).astype(f)[:, None],
        np.where(r < W - 1, 0.0, HUGE).astype(f)[:, None], pads.astype(f)[:, None],
        np.eye(P, dtype=f), np.where(inside, 0.0, MASKED).astype(f), np.zeros((P, 6), f)], axis=1)
    rows = np.concatenate([a("L0_xattn_bv"), a("L0_xattn_bo"), a("L0_ffn_expert_bias"),
                           np.stack([a("g_xattn")[0], a("g_xattn")[1], a("g_ffn")[0], a("g_ffn")[1]])])
    b2 = np.concatenate([a("L0_ffn_rb2"), a("L0_ffn_sb2")[None]])
    ctxT = a("ctx_1024").reshape(B, S, KC, P).transpose(0, 3, 2, 1)
    at = r[:, None] - r[None, :] + a("L1_xattn_rel_emb").shape[0] // 2
    by_unit = np.arange(H).reshape(KC, NU, 2).transpose(1, 0, 2).reshape(-1)
    rel = a("L1_xattn_rel_emb")[at].transpose(0, 2, 1)[:, by_unit]
    rhsT = a("L1_ffn_rhs").T.reshape(KC, P, D).transpose(1, 0, 2)
    mask = a("mask_Bx1xSxS2_bf1").reshape(B, S, S).view(np.uint8)
    return {"x": a("x"), "ctxT": ctxT, "mask": mask, "weights": weights, "cols": cols, "rows": rows, "b2": b2,
            "rel": rel, "rhsT": rhsT}


def kernel(**inputs):
    import numpy as _np
    import concourse.bacc as _bacc
    from concourse import mybir as _mybir
    from concourse.bass_utils import run_bass_kernel_spmd as _run

    nc = _bacc.Bacc("TRN2", target_bir_lowering=False, num_devices=1)
    arrays, args = {}, []
    laid = lay_out(inputs)
    for name in _INS:
        v = _np.ascontiguousarray(laid[name])
        arrays[f"in_{name}_dram"] = v
        args.append(nc.dram_tensor(f"in_{name}_dram", v.shape, _mybir.dt.from_np(v.dtype), kind="ExternalInput").ap())
    args.append(nc.dram_tensor("out_0_dram", (B, S, D), _mybir.dt.float32, kind="ExternalOutput").ap())
    build(nc, *args)
    r = _run(nc, [arrays], core_ids=[0])
    return r.results[0]["out_0_dram"]
```

```python
from contextlib import ExitStack

import concourse.bass as bass
from concourse import mybir

P = 128
F32 = mybir.dt.float32
BF16 = mybir.dt.bfloat16
U8 = mybir.dt.uint8
ALU = mybir.AluOpType
ACT = mybir.ActivationFunctionType
AX_X = mybir.AxisListType.X

B, S, D = 16, 128, 256
H = 16
HD = D // H
W = 16
KC = D // P
E = 8
HID = 128
EPS = 1e-5
SCALE = HD ** -0.5
MASKED = -float(2 ** 100)
HUGE = 3.0e38
ROUND = 1.5 * 2 ** 23
UH = 4
NU = H // UH
UW = UH * S

ATT_W = 4 * KC * D
NE = E + 1
W1_W = NE * KC * HID
W2_W = NE * D


def column_consts():
    at, n = {}, 0
    for name, w in (("bq", KC), ("bk", KC), ("b1", NE), ("rw", KC * E), ("even", 1), ("odd", 1),
                    ("ncap", 1), ("npad", 1), ("ident", P), ("band", S), ("minus", 6)):
        at[name] = slice(n, n + w)
        n += w
    return at, n


COL, NCOL = column_consts()


def row_consts():
    at, n = {}, 0
    for name, w in (("bv", D), ("bo", D), ("eb", E), ("g", 4)):
        at[name] = slice(n, n + w)
        n += w
    return at, n


ROW, NROW = row_consts()
LAG = 5
PROLOGUE, STEPS = (LAG + 3) // 2 * 2, B + LAG


def build(nc, x, ctxT, mask, weights, cols, rows, b2, rel, rhsT, out):
    with ExitStack() as ctx:
        def sb(name, shape, dt=F32):
            return ctx.enter_context(nc.sbuf_tensor(name, shape, dt))

        def ps(name, shape=(P, 512), dt=F32):
            return ctx.enter_context(nc.psum_tensor(name, list(shape), dt))

        def sem(name):
            return ctx.enter_context(nc.semaphore(name))

        NW = 2 * ATT_W + W1_W + W2_W
        w_sb = sb("w_sb", [P, NW])
        col = sb("col", [P, NCOL])
        row = sb("row", [P, NROW])
        b2_sb = sb("b2_sb", [NE, D])
        rel_sb = sb("rel_sb", [P, H, S])
        bqs = sb("bqs", [P, KC])
        gate = sb("gate", [P, 4])
        gbo = sb("gbo", [P, D])
        half = sb("half", [P, E])
        minus_half = sb("minus_half", [P, 1])
        ident_b = sb("ident_b", [P, P], BF16)
        rhs_raw = sb("rhs_raw", [P, KC, D])
        rhs_am = sb("rhs_am", [P, 4 * KC])
        rhs_qT = sb("rhs_qT", [P, KC, D])
        rhs_q = sb("rhs_q", [P, KC, D], BF16)
        rhs_sc = sb("rhs_sc", [P, D])
        ident = col[:, COL["ident"]]
        band = col[:, COL["band"]]

        def csl(name, i=0, n=1):
            a = COL[name].start + i
            return col[:, a:a + n]

        class Norm:
            def __init__(self, n, bank):
                self.stat = sb(f"{n}_stat", [P, 6])
                self.mv = sb(f"{n}_mv", [P, 2])
                self.ve = sb(f"{n}_ve", [P, 1])
                self.rstd = sb(f"{n}_rstd", [P, 1])
                self.xn = sb(f"{n}_xn", [P, D])
                self.xt = sb(f"{n}_xt", [P, KC, S])
                self.bank = bank
                self.stat_ready = sem(f"{n}_stat_ready")
                self.mv_ready = sem(f"{n}_mv_ready")
                self.ve_ready = sem(f"{n}_ve_ready")
                self.rstd_ready = sem(f"{n}_rstd_ready")
                self.xn_ready = sem(f"{n}_xn_ready")
                self.xt_ready = sem(f"{n}_xt_ready")
                self.xt_done = sem(f"{n}_xt_done")

        class Attention:
            def __init__(self, n, which):
                self.which = which
                self.X, self.Y, self.Z = ps(f"{n}_X"), ps(f"{n}_Y"), ps(f"{n}_Z")
                self.norm = Norm(n, self.Z)
                self.w = which * ATT_W
                self.ctx = [sb(f"{n}_ctx{i}", [P, KC, S]) for i in range(2)]
                self.q = sb(f"{n}_q", [P, KC, S])
                self.k = sb(f"{n}_k", [P, KC, 2, S])
                self.v = sb(f"{n}_v", [P, H, HD + 1])
                self.t = sb(f"{n}_t", [P, NU, UH, S])
                self.nm = sb(f"{n}_nm", [P, H])
                self.nmc = sb(f"{n}_nmc", [P, H]) if which == 0 else self.nm
                self.p = self.t
                self.pt = sb(f"{n}_pt", [P, NU, UH, S])
                self.e0a = sb(f"{n}_e0a", [P, H])
                self.e0 = sb(f"{n}_e0", [P, H])
                self.den = sb(f"{n}_den", [P, H])
                self.rden = sb(f"{n}_rden", [P, H])
                self.o = sb(f"{n}_o", [P, H, HD])
                self.ot = sb(f"{n}_ot", [P, KC, S])
                self.ctx_in = [sem(f"{n}_ctx_in{i}") for i in range(2)]
                for_each = ("qk_ready v_ready q_done k_done v_done s_ready t_ready "
                            "nm_ready nmc_ready sub_done p_ready pt_ready pt_done av_ready e0a_ready e0_ready "
                            "den_ready rden_ready o_ready ot_ready ot_done y_ready x_done").split()
                (self.qk_ready, self.v_ready, self.q_done, self.k_done,
                 self.v_done, self.s_ready, self.t_ready, self.nm_ready, self.nmc_ready, self.sub_done,
                 self.p_ready, self.pt_ready, self.pt_done, self.av_ready, self.e0a_ready, self.e0_ready,
                 self.den_ready, self.rden_ready, self.o_ready, self.ot_ready, self.ot_done,
                 self.y_ready, self.x_done) = [sem(f"{n}_{k}") for k in for_each]
                if which == 0:
                    self.xb_ready = sem(f"{n}_xb_ready")

            def bank(self, u):
                return (self.X, self.Y)[u % 2]

        A0, A1 = Attention("a0", 0), Attention("a1", 1)

        x0 = [sb(f"x0_{i}", [P, D]) for i in range(2)]
        x0b = sb("x0b", [P, D])
        x1 = [sb(f"x1_{i}", [P, D]) for i in range(2)]
        x2 = [sb(f"x2_{i}", [P, D]) for i in range(2)]
        x3 = sb("x3", [P, D])
        y_sb = [sb(f"y_{i}", [P, D]) for i in range(2)]
        mask_u8 = [sb(f"mask_u8_{i}", [P, S], U8) for i in range(2)]
        mask_neg = sb("mask_neg", [P, S])
        bm = sb("bm", [P, H, S])

        F0, F1 = ps("F0"), ps("F1")
        FN = Norm("f", F0)
        lg, lab, lex, lln, lsp = (sb(n, [P, E]) for n in ("lg", "lab", "lex", "lln", "lsp"))
        act14 = sb("act14", [P, E + 6])
        mx8 = sb("mx8", [P, 8])
        rep8 = sb("rep8", [P, 8])
        zap = sb("zap", [P, E + 6])
        cf9 = sb("cf9", [P, NE])
        cfg = sb("cfg", [P, E])
        cfT = sb("cfT", [NE, S])
        h = sb("h", [P, NE, S])
        acc = [sb(f"acc_{i}", [P, D]) for i in range(2)]
        HU = [(0, 4), (4, 8), (8, 9)]
        (lgm_ready, lg_ready, lab_ready, lex_ready, lln_ready, lsp_ready, act_ready, mx_ready, rep_ready,
         zap_ready, cf_ready, cfg_ready, cft_ready, cft_done, hm_ready, h_ready, ym_ready,
         acc_ready) = [sem(n) for n in (
             "lgm_ready lg_ready lab_ready lex_ready lln_ready lsp_ready act_ready mx_ready rep_ready "
             "zap_ready cf_ready cfg_ready cft_ready cft_done hm_ready h_ready ym_ready "
             "acc_ready").split()]

        QN = Norm("q", None)
        am = sb("am", [P, 1])
        lsc = sb("lsc", [P, 1])
        rsc = sb("rsc", [P, 1])
        qf = sb("qf", [P, D])
        qc = sb("qc", [P, D])
        qb = sb("qb", [P, D], BF16)
        qT = sb("qT", [P, KC, S], BF16)
        qy = sb("qy", [P, D])
        (am_ready, lsc_ready, rsc_ready, qf_ready, qc_ready, qb_ready, qt_ready, qt_done, qm_ready, qy_ready,
         y_ready) = [sem(n) for n in (
             "am_ready lsc_ready rsc_ready qf_ready qc_ready qb_ready qt_ready qt_done qm_ready qy_ready "
             "y_ready").split()]

        x_in = [sem(f"x_in{i}") for i in range(2)]
        mask_in = [sem(f"mask_in{i}") for i in range(2)]
        y_out = [sem(f"y_out{i}") for i in range(2)]
        mneg_ready, bm_ready = sem("mneg_ready"), sem("bm_ready")
        w_in, c_in, gtanh = sem("w_in"), sem("c_in"), sem("gtanh")
        pool_set, act_set, dve_set = sem("pool_set"), sem("act_set"), sem("dve_set")
        r_t, r_q, r_s = sem("r_t"), sem("r_q"), sem("r_s")
        waits_apart = sem("waits_apart")


        def upto(eng, s, b, per=1, k=None):
            eng.wait_ge(s, b * per + (per if k is None else k))

        def before(eng, s, b, per=1, k=None):
            n = b * per + (per if k is None else k) - per
            if type(n) is not int or n > 0:
                eng.wait_ge(s, n)

        def before2(eng, s, b, per=1, k=None):
            n = b * per + (per if k is None else k) - 2 * per
            if type(n) is not int or n > 0:
                eng.wait_ge(s, n)

        def dma_nth(b, par):
            return (b - par) * 8 + 16

        def settled(eng):
            eng.wait_ge(pool_set, 7)
            eng.wait_ge(act_set, 1)
            eng.wait_ge(dve_set, 2)

        def apart(eng):
            eng.sem_inc(waits_apart, 1)

        def unit_heads(t, u):
            return t[:, :].rearrange("p (c u j) -> p c u j", c=KC, u=NU)[:, :, u, :]

        def run(eng, step):
            for s in range(PROLOGUE):
                step(s, s % 2)
            with eng.Fori(PROLOGUE // 2, B // 2, 1) as turn_:
                step(turn_ * 2, 0)
                step(turn_ * 2 + 1, 1)
            for s in range(B, STEPS):
                step(s, s % 2)

        def at(s, par, lag, part, *what):
            if type(s) is not int or 0 <= s - lag < B:
                part(s - lag, (par + lag) % 2, *what)

        def wslice(off, k, m0, m, width):
            a = off + k * width + m0
            return w_sb[:, a:a + m]

        block = ctx.enter_context(nc.Block())

        @block.sync
        def _(sp):
            sp.dma_start(col[:, :], cols).then_inc(c_in, 16)
            sp.dma_start(row[:, :], rows.partition_broadcast(P)).then_inc(c_in, 16)
            sp.dma_start(b2_sb[:, :], b2).then_inc(c_in, 16)
            sp.dma_start(rhs_raw[:, :, :], rhsT).then_inc(c_in, 16)
            sp.dma_start(rel_sb[:, :, :], rel).then_inc(c_in, 16)
            sp.dma_start(w_sb[:, :], weights).then_inc(w_in, 16)

            def load_x(b, par):
                before2(sp, A0.xb_ready, b)
                before2(sp, A0.norm.xn_ready, b)
                apart(sp)
                sp.dma_start(x0[par][:, :], x[b]).then_inc(x_in[par], 16)

            def load_ctx(b, par, A):
                before2(sp, A.v_ready, b)
                before2(sp, A.qk_ready, b)
                apart(sp)
                sp.dma_start(A.ctx[par][:, :, :], ctxT[b]).then_inc(A.ctx_in[par], 16)

            def load_mask(b, par):
                before2(sp, mneg_ready, b)
                apart(sp)
                sp.dma_start(mask_u8[par][:, :], mask[b]).then_inc(mask_in[par], 16)

            def store(b, par):
                upto(sp, y_ready, b)
                apart(sp)
                sp.dma_start(out[b], y_sb[par][:, :]).then_inc(y_out[par], 16)

            def step(s, par):
                at(s, par, 2, load_ctx, A0)
                at(s, par, 2, load_x)
                at(s, par, 4, load_mask)
                at(s, par, 4, load_ctx, A1)
                at(s, par, 5, store)

            run(sp, step)
            for i in range(2):
                sp.wait_ge(y_out[i], 16 * (B // 2))

        @block.gpsimd
        def _(pool):
            g = nc.gpsimd
            pool.wait_ge(c_in, 80)
            g.memset(half[:, :], 0.5).then_inc(pool_set, 1)
            g.memset(minus_half[:, :], -0.5).then_inc(pool_set, 1)
            g.memset(A0.v[:, :, HD:HD + 1], 1.0).then_inc(pool_set, 1)
            g.memset(A1.v[:, :, HD:HD + 1], 1.0).then_inc(pool_set, 1)
            g.memset(rep8[:, :], -1.0).then_inc(pool_set, 1)
            g.memset(cf9[:, :], 1.0).then_inc(pool_set, 1)
            g.memset(act14[:, :], -1.0).then_inc(pool_set, 1)

            def rstd(b, par, N):
                upto(pool, N.mv_ready, b)
                apart(pool)
                g.tensor_scalar(N.ve[:, :], N.mv[:, 1:2], EPS, None, ALU.add).then_inc(N.ve_ready, 1)
                upto(pool, N.ve_ready, b)
                before(pool, N.xn_ready, b)
                g.tensor_tensor(N.rstd[:, :], N.ve[:, :], minus_half[:, :], ALU.pow).then_inc(N.rstd_ready, 1)

            def add_bo(b, par):
                pool.wait_ge(x_in[par], dma_nth(b, par))
                before(pool, A0.x_done, b)
                g.tensor_tensor(x0b[:, :], x0[par][:, :], gbo[:, :], ALU.add).then_inc(A0.xb_ready, 1)

            def bias_mask(b, par):
                pool.wait_ge(mask_in[par], dma_nth(b, par))
                before(pool, bm_ready, b, NU)
                apart(pool)
                g.tensor_scalar(mask_neg[:, :], mask_u8[par][:, :], 0.0, MASKED, ALU.is_equal,
                                ALU.mult).then_inc(mneg_ready, 1)
                upto(pool, mneg_ready, b)
                for u in range(NU):
                    before(pool, A1.t_ready, b, NU, u + 1)
                    g.tensor_tensor(bm[:, UH * u:UH * (u + 1), :], rel_sb[:, UH * u:UH * (u + 1), :],
                                    mask_neg[:, None, :].to_broadcast([P, UH, S]),
                                    ALU.add).then_inc(bm_ready, 1)

            def subtract(b, par, A, u):
                upto(pool, A.nmc_ready if A.which == 0 else A.nm_ready, b, NU, u + 1)
                t4 = A.t[:, u, :, :].rearrange("p (c j) t -> p c j t", c=KC)
                g.tensor_tensor(t4, t4, unit_heads(A.nmc, u)[:, :, :, None].to_broadcast([P, KC, 2, S]),
                                ALU.add).then_inc(A.sub_done, 1)

            def activation_root(b, par):
                upto(pool, lsp_ready, b)
                before(pool, cf_ready, b)
                g.tensor_tensor(act14[:, 0:E], lsp[:, :], half[:, :], ALU.pow).then_inc(act_ready, 1)

            def step(s, par):
                at(s, par, 4, subtract, A1, 1)
                at(s, par, 3, activation_root)
                at(s, par, 4, subtract, A1, 2)
                at(s, par, 4, subtract, A1, 3)
                at(s, par, 2, subtract, A0, 3)
                at(s, par, 3, bias_mask)
                at(s, par, 1, rstd, A0.norm)
                at(s, par, 2, add_bo)
                at(s, par, 3, rstd, A1.norm)
                at(s, par, 4, rstd, QN)
                at(s, par, 2, rstd, FN)
                at(s, par, 1, subtract, A0, 0)
                at(s, par, 1, subtract, A0, 1)
                at(s, par, 3, subtract, A1, 0)
                at(s, par, 1, subtract, A0, 2)

            settled(pool)
            run(pool, step)

        @block.scalar
        def _(act):
            a = nc.scalar
            act.wait_ge(c_in, 80)
            a.activation(gate[:, :], row[:, ROW["g"]], ACT.Tanh).then_inc(gtanh, 1)
            a.activation(bqs[:, :], col[:, COL["bq"]], ACT.Copy, scale=SCALE).then_inc(act_set, 1)
            settled(act)

            def xt_out(b, par, N, readers, per):
                upto(act, N.xt_ready, b)
                before(act, readers, b, per)
                a.activation(N.xt[:, :, :], N.bank[:, 0:D].rearrange("p (c t) -> p c t", c=KC),
                             ACT.Copy).then_inc(N.xt_done, 1)

            def q_out(b, par, A):
                upto(act, A.qk_ready, b)
                before(act, A.s_ready, b, NU)
                if A.which == 0:
                    for c in range(KC):
                        i = a.activation(A.q[:, c, :], A.X[:, c * S:(c + 1) * S], ACT.Identity,
                                         bias=bqs[:, c:c + 1], scale=SCALE)
                    i.then_inc(A.q_done, 1)
                else:
                    a.activation(A.q[:, :, :], A.X[:, 0:D].rearrange("p (c t) -> p c t", c=KC), ACT.Copy,
                                 scale=SCALE).then_inc(A.q_done, 1)

            def v_out1(b, par):
                upto(act, A1.v_ready, b)
                before(act, A1.av_ready, b, NU)
                a.activation(A1.v[:, :, 0:HD], A1.Y[:, 0:D].rearrange("p (h d) -> p h d", h=H),
                             ACT.Copy).then_inc(A1.v_done, 1)

            def exps(b, par, A, u):
                upto(act, A.sub_done, b, NU, u + 1)
                a.activation(A.p[:, u, :, :], A.t[:, u, :, :], ACT.Exp).then_inc(A.p_ready, 1)

            def pt_out(b, par, A, u):
                upto(act, A.pt_ready, b, NU, u + 1)
                before(act, A.av_ready, b, NU, u + 1)
                a.activation(A.pt[:, u, :, :], A.Z[:, :].rearrange("p (h t) -> p h t", h=UH),
                             ACT.Copy).then_inc(A.pt_done, 1)

            def pad_weight(b, par):
                upto(act, A0.e0a_ready, b)
                before(act, A0.den_ready, b)
                a.activation(A0.e0[:, :], A0.e0a[:, :], ACT.Exp).then_inc(A0.e0_ready, 1)

            def ot_out(b, par, A):
                upto(act, A.ot_ready, b)
                before(act, A.y_ready, b)
                a.activation(A.ot[:, :, :], A.Y[:, 0:D].rearrange("p (c t) -> p c t", c=KC),
                             ACT.Copy).then_inc(A.ot_done, 1)

            def softplus_log(b, par):
                upto(act, lab_ready, b)
                before(act, lln_ready, b)
                a.activation(lex[:, :], lab[:, :], ACT.Exp, scale=-1.0).then_inc(lex_ready, 1)
                upto(act, lex_ready, b)
                before(act, lsp_ready, b)
                a.activation(lln[:, :], lex[:, :], ACT.Ln, bias=1.0).then_inc(lln_ready, 1)

            def cft_out(b, par):
                upto(act, cft_ready, b)
                before(act, ym_ready, b, 5)
                a.activation(cfT[:, :], F1[0:NE, 0:S], ACT.Copy).then_inc(cft_done, 1)

            def silus(b, par, i):
                upto(act, hm_ready, b, len(HU), i + 1)
                before(act, ym_ready, b, 5)
                lo, hi = HU[i]
                for e in range(lo, hi):
                    n = a.activation(h[:, e, :], (F0, F1)[i % 2][:, (e - lo) * S:(e - lo + 1) * S], ACT.Silu,
                                     bias=csl("b1", e))
                n.then_inc(h_ready, 1)

            def qt_out(b, par):
                upto(act, qt_ready, b)
                before(act, qm_ready, b)
                a.activation(qT[:, :, :], A1.Z[:, 0:D // 2].bitcast(BF16).rearrange("p (c t) -> p c t", c=KC),
                             ACT.Copy).then_inc(qt_done, 1)

            def step(s, par):
                at(s, par, 1, xt_out, A0.norm, A0.qk_ready, 1)
                at(s, par, 1, q_out, A0)
                at(s, par, 4, qt_out)
                at(s, par, 3, xt_out, A1.norm, A1.qk_ready, 1)
                at(s, par, 3, q_out, A1)
                at(s, par, 2, xt_out, FN, hm_ready, len(HU))
                at(s, par, 3, v_out1)
                at(s, par, 1, exps, A0, 0)
                at(s, par, 2, softplus_log)
                at(s, par, 1, exps, A0, 1)
                at(s, par, 3, exps, A1, 0)
                at(s, par, 1, pt_out, A0, 0)
                at(s, par, 3, exps, A1, 1)
                at(s, par, 3, pt_out, A1, 0)
                at(s, par, 1, exps, A0, 2)
                at(s, par, 3, pt_out, A1, 1)
                at(s, par, 1, pt_out, A0, 1)
                at(s, par, 3, exps, A1, 2)
                at(s, par, 2, cft_out)
                at(s, par, 3, pt_out, A1, 2)
                at(s, par, 1, pt_out, A0, 2)
                at(s, par, 1, pad_weight)
                at(s, par, 3, exps, A1, 3)
                at(s, par, 1, exps, A0, 3)
                at(s, par, 2, silus, 0)
                at(s, par, 2, silus, 1)
                at(s, par, 3, pt_out, A1, 3)
                at(s, par, 1, pt_out, A0, 3)
                at(s, par, 2, silus, 2)
                at(s, par, 1, ot_out, A0)
                at(s, par, 3, ot_out, A1)

            run(act, step)

        @block.vector
        def _(dve):
            v = nc.vector
            dve.wait_ge(c_in, 80)
            v.tensor_copy(ident_b[:, :], ident).then_inc(dve_set, 1)
            dve.wait_ge(gtanh, 1)
            v.tensor_scalar(gbo[:, :], row[:, ROW["bo"]], gate[:, 0:1], None, ALU.mult).then_inc(dve_set, 1)
            for c in range(KC):
                i = v.tensor_reduce(rhs_am[:, c:c + 1], rhs_raw[:, c, :], AX_X, ALU.max, apply_absolute_value=True)
            i.then_inc(r_s, 1)
            dve.wait_ge(r_s, 1)
            v.tensor_scalar(rhs_am[:, 2:4], rhs_am[:, 0:2], 1e-12, 1.0 / 127.0, ALU.max, ALU.mult).then_inc(r_s, 1)
            dve.wait_ge(r_s, 2)
            v.reciprocal(rhs_am[:, 4:6], rhs_am[:, 2:4]).then_inc(r_s, 1)
            dve.wait_ge(r_s, 3)
            for c in range(KC):
                i = v.tensor_scalar(rhs_qT[:, c, :], rhs_raw[:, c, :], rhs_am[:, 4 + c:5 + c], ROUND,
                                    ALU.mult, ALU.add)
            i.then_inc(r_q, 1)
            dve.wait_ge(r_q, 1)
            v.tensor_scalar(rhs_qT[:, :, :], rhs_qT[:, :, :], ROUND + 127.0, ROUND - 127.0, ALU.min,
                            ALU.max).then_inc(r_q, 1)
            dve.wait_ge(r_q, 2)
            v.tensor_scalar(rhs_qT[:, :, :], rhs_qT[:, :, :], ROUND, None, ALU.subtract).then_inc(r_q, 1)
            dve.wait_ge(r_t, 1)
            v.tensor_copy(rhs_q[:, :, :], A0.X[:, :].rearrange("p (k n) -> p k n", k=KC)).then_inc(r_q, 1)
            v.tensor_copy(rhs_sc[:, :], A0.Y[:, 0:D]).then_inc(r_q, 1)
            settled(dve)

            def source(b, par, N):
                if N is A0.norm:
                    return x0[par], x_in[par], dma_nth(b, par)
                if N is FN:
                    return x1[par], A0.x_done, b + 1
                if N is A1.norm:
                    return x2[par], acc_ready, b * NE + NE
                return x3, A1.x_done, b + 1

            def stats(b, par, N):
                src, ready, n = source(b, par, N)
                dve.wait_ge(ready, n)
                if N.bank is not None:
                    before(dve, N.xn_ready, b)
                v.bn_stats(N.stat[:, :], src[:, :]).then_inc(N.stat_ready, 1)
                upto(dve, N.stat_ready, b)
                apart(dve)
                v.bn_aggr(N.mv[:, :], N.stat[:, :]).then_inc(N.mv_ready, 1)

            def normalise(b, par, N):
                upto(dve, N.rstd_ready, b)
                if N.bank is not None:
                    before(dve, N.xt_ready, b)
                v.tensor_scalar(N.xn[:, :], source(b, par, N)[0][:, :], N.mv[:, 0:1], N.rstd[:, 0:1], ALU.subtract,
                                ALU.mult).then_inc(N.xn_ready, 1)

            def k_out(b, par, A):
                upto(dve, A.q_done, b)
                before(dve, A.s_ready, b, NU)
                for j, m in enumerate(("even", "odd")):
                    if A.which == 0:
                        for c in range(KC):
                            i = v.tensor_scalar(A.k[:, c, j, :], A.X[:, D + c * S:D + (c + 1) * S], csl("bk", c),
                                                csl(m), ALU.add, ALU.mult)
                    else:
                        i = v.tensor_scalar(A.k[:, :, j, :], A.X[:, D:2 * D].rearrange("p (c t) -> p c t", c=KC),
                                            csl(m), None, ALU.mult)
                i.then_inc(A.k_done, 1)

            def v_out0(b, par):
                upto(dve, A0.v_ready, b)
                before(dve, A0.av_ready, b, NU)
                v.tensor_tensor(A0.v[:, :, 0:HD], A0.Y[:, 0:D].rearrange("p (h d) -> p h d", h=H),
                                row[:, ROW["bv"]].rearrange("p (h d) -> p h d", h=H),
                                ALU.add).then_inc(A0.v_done, 1)

            def maxima(b, par, A, u):
                upto(dve, A.s_ready, b, NU, u + 1)
                before(dve, A.pt_ready, b, NU, u + 1)
                if A.which == 0:
                    add = band[:, None, :].to_broadcast([P, UH, S])
                else:
                    upto(dve, bm_ready, b, NU, u + 1)
                    add = bm[:, UH * u:UH * (u + 1), :]
                v.tensor_tensor(A.t[:, u, :, :], A.bank(u)[:, :].rearrange("p (h t) -> p h t", h=UH), add,
                                ALU.add).then_inc(A.t_ready, 1)
                upto(dve, A.t_ready, b, NU, u + 1)
                before(dve, A.sub_done, b, NU, u + 1)
                v.tensor_reduce(unit_heads(A.nm, u), A.t[:, u, :, :].rearrange("p (c j) t -> p c j t", c=KC),
                                AX_X, ALU.max, negate=True).then_inc(A.nm_ready, 1)
                if A.which == 0:
                    upto(dve, A.nm_ready, b, NU, u + 1)
                    if u == 0:
                        before(dve, A.e0a_ready, b)
                    v.tensor_scalar(unit_heads(A.nmc, u), unit_heads(A.nm, u), csl("ncap"), None, ALU.min).then_inc(A.nmc_ready, 1)

            def pad_argument(b, par):
                upto(dve, A0.nmc_ready, b, NU)
                before(dve, A0.e0_ready, b)
                v.tensor_scalar(A0.e0a[:, :], A0.nmc[:, :], 0.0, None, ALU.min).then_inc(A0.e0a_ready, 1)

            def heads_out(b, par, A):
                upto(dve, A.av_ready, b, NU)
                av = A.X[:, 0:H * (HD + 1)].rearrange("p (h d) -> p h d", h=H)
                if A.which == 0:
                    upto(dve, A.e0_ready, b)
                    before(dve, A.rden_ready, b)
                    v.scalar_tensor_tensor(out=A.den[:, :], in0=A.e0[:, :], scalar=csl("npad"), in1=av[:, :, HD],
                                           op0=ALU.mult, op1=ALU.add).then_inc(A.den_ready, 1)
                    upto(dve, A.den_ready, b)
                    before(dve, A.o_ready, b)
                    v.reciprocal(A.rden[:, :], A.den[:, :]).then_inc(A.rden_ready, 1)
                else:
                    before(dve, A.o_ready, b)
                    v.reciprocal(A.rden[:, :], av[:, :, HD]).then_inc(A.rden_ready, 1)
                upto(dve, A.rden_ready, b)
                before(dve, A.ot_ready, b)
                v.tensor_tensor(A.o[:, :, :], av[:, :, 0:HD], A.rden[:, :, None].to_broadcast([P, H, HD]),
                                ALU.mult).then_inc(A.o_ready, 1)

            def residual0(b, par):
                upto(dve, A0.y_ready, b)
                upto(dve, A0.xb_ready, b)
                before2(dve, acc_ready, b, NE)
                v.scalar_tensor_tensor(out=x1[par][:, :], in0=A0.Z[:, 0:D], scalar=gate[:, 0:1], in1=x0b[:, :],
                                       op0=ALU.mult, op1=ALU.add).then_inc(A0.x_done, 1)

            def residual1(b, par):
                upto(dve, A1.y_ready, b)
                before(dve, y_ready, b)
                v.scalar_tensor_tensor(out=x3[:, :], in0=A1.Z[:, 0:D], scalar=gate[:, 1:2], in1=x2[par][:, :],
                                       op0=ALU.mult, op1=ALU.add).then_inc(A1.x_done, 1)

            def router(b, par):
                upto(dve, lgm_ready, b)
                before(dve, lsp_ready, b)
                v.tensor_tensor(lg[:, :], F1[:, 0:E], row[:, ROW["eb"]], ALU.add).then_inc(lg_ready, 1)
                upto(dve, lg_ready, b)
                before(dve, lex_ready, b)
                v.scalar_tensor_tensor(out=lab[:, :], in0=lg[:, :], scalar=-1.0, in1=lg[:, :], op0=ALU.mult,
                                       op1=ALU.max).then_inc(lab_ready, 1)

            def softplus(b, par):
                upto(dve, lln_ready, b)
                before(dve, act_ready, b)
                v.scalar_tensor_tensor(out=lsp[:, :], in0=lg[:, :], scalar=0.0, in1=lln[:, :], op0=ALU.max,
                                       op1=ALU.add).then_inc(lsp_ready, 1)

            def top_two(b, par):
                upto(dve, act_ready, b)
                before(dve, rep_ready, b)
                apart(dve)
                v.max(mx8[:, :], act14[:, 0:E]).then_inc(mx_ready, 1)
                upto(dve, mx_ready, b)
                before(dve, zap_ready, b)
                v.tensor_copy(rep8[:, 0:2], mx8[:, 0:2]).then_inc(rep_ready, 1)
                upto(dve, rep_ready, b)
                before(dve, cf_ready, b)
                apart(dve)
                v.match_replace(zap[:, :], rep8[:, :], act14[:, :], 0.0).then_inc(zap_ready, 1)
                upto(dve, zap_ready, b)
                before(dve, cft_ready, b)
                before(dve, cfg_ready, b)
                v.tensor_tensor(cf9[:, 0:E], act14[:, 0:E], zap[:, 0:E], ALU.subtract).then_inc(cf_ready, 1)
                upto(dve, cf_ready, b)
                before(dve, acc_ready, b, NE)
                v.tensor_scalar(cfg[:, :], cf9[:, 0:E], gate[:, 2:3], None, ALU.mult).then_inc(cfg_ready, 1)

            def add_shared(b, par):
                upto(dve, ym_ready, b, 5, 1)
                v.scalar_tensor_tensor(out=acc[0][:, :], in0=F1[:, 0:D], scalar=gate[:, 2:3], in1=x1[par][:, :],
                                       op0=ALU.mult, op1=ALU.add).then_inc(acc_ready, 1)

            def add_pair(b, par, j):
                if j == 0:
                    upto(dve, cfg_ready, b)
                upto(dve, ym_ready, b, 5, 2 + j)
                bank = (F0, F1)[j % 2]
                for e in (2 * j, 2 * j + 1):
                    upto(dve, acc_ready, b, NE, e + 1)
                    if e == E - 1:
                        before2(dve, A1.x_done, b)
                    v.scalar_tensor_tensor(out=x2[par][:, :] if e == E - 1 else acc[(e + 1) % 2][:, :],
                                           in0=bank[:, (e % 2) * D:(e % 2 + 1) * D], scalar=cfg[:, e:e + 1],
                                           in1=acc[e % 2][:, :], op0=ALU.mult, op1=ALU.add).then_inc(acc_ready, 1)

            def quantise(b, par):
                upto(dve, QN.xn_ready, b)
                before(dve, lsc_ready, b)
                v.tensor_reduce(am[:, :], QN.xn[:, :], AX_X, ALU.max, apply_absolute_value=True).then_inc(am_ready, 1)
                upto(dve, am_ready, b)
                before(dve, qy_ready, b)
                v.tensor_scalar(lsc[:, :], am[:, :], 1e-12, 1.0 / 127.0, ALU.max, ALU.mult).then_inc(lsc_ready, 1)
                upto(dve, lsc_ready, b)
                v.reciprocal(rsc[:, :], lsc[:, :]).then_inc(rsc_ready, 1)
                upto(dve, rsc_ready, b)
                v.tensor_scalar(qf[:, :], QN.xn[:, :], rsc[:, 0:1], ROUND, ALU.mult, ALU.add).then_inc(qf_ready, 1)
                upto(dve, qf_ready, b)
                v.tensor_scalar(qc[:, :], qf[:, :], ROUND + 127.0, ROUND - 127.0, ALU.min,
                                ALU.max).then_inc(qc_ready, 1)
                upto(dve, qc_ready, b)
                before(dve, qt_ready, b)
                v.tensor_scalar(qb[:, :], qc[:, :], ROUND, None, ALU.subtract).then_inc(qb_ready, 1)

            def final(b, par):
                upto(dve, qm_ready, b)
                v.scalar_tensor_tensor(out=qy[:, :], in0=A1.X[:, 0:D], scalar=lsc[:, 0:1], in1=rhs_sc[:, :],
                                       op0=ALU.mult, op1=ALU.mult).then_inc(qy_ready, 1)
                upto(dve, qy_ready, b)
                n = dma_nth(b, par) - 16
                if type(n) is not int or n > 0:
                    dve.wait_ge(y_out[par], n)
                v.scalar_tensor_tensor(out=y_sb[par][:, :], in0=qy[:, :], scalar=gate[:, 3:4], in1=x3[:, :],
                                       op0=ALU.mult, op1=ALU.add).then_inc(y_ready, 1)

            def step(s, par):
                at(s, par, 4, stats, QN)
                at(s, par, 2, stats, FN)
                at(s, par, 4, normalise, QN)
                at(s, par, 4, quantise)
                at(s, par, 3, normalise, A1.norm)
                at(s, par, 1, k_out, A0)
                at(s, par, 2, normalise, FN)
                at(s, par, 4, final)
                at(s, par, 1, v_out0)
                at(s, par, 1, maxima, A0, 0)
                at(s, par, 3, k_out, A1)
                at(s, par, 1, maxima, A0, 1)
                at(s, par, 2, router)
                at(s, par, 3, maxima, A1, 0)
                at(s, par, 1, maxima, A0, 2)
                at(s, par, 3, maxima, A1, 1)
                at(s, par, 2, softplus)
                at(s, par, 3, maxima, A1, 2)
                at(s, par, 0, stats, A0.norm)
                at(s, par, 1, maxima, A0, 3)
                at(s, par, 2, top_two)
                at(s, par, 3, maxima, A1, 3)
                at(s, par, 1, pad_argument)
                at(s, par, 2, add_shared)
                at(s, par, 1, heads_out, A0)
                at(s, par, 2, add_pair, 0)
                at(s, par, 2, add_pair, 1)
                at(s, par, 3, heads_out, A1)
                at(s, par, 2, add_pair, 2)
                at(s, par, 2, add_pair, 3)
                at(s, par, 0, normalise, A0.norm)
                at(s, par, 2, stats, A1.norm)
                at(s, par, 3, residual1)
                at(s, par, 1, residual0)

            run(dve, step)

        @block.tensor
        def _(pe):
            t = nc.tensor

            pe.wait_ge(c_in, 80)
            pe.wait_ge(r_q, 3)
            for k in range(KC):
                for n in range(KC):
                    t.transpose(A0.X[:, k * D + n * P:k * D + (n + 1) * P], rhs_qT[:, n, k * P:(k + 1) * P], ident)
            for n in range(KC):
                i = t.matmul(A0.Y[:, n * P:(n + 1) * P], rhs_am[:, 2 + n:3 + n].to_broadcast([P, P]), ident,
                             start=True, stop=True)
            i.then_inc(r_t, 1)
            pe.wait_ge(r_q, 5)
            pe.wait_ge(w_in, 16)
            settled(pe)

            def norm_t(b, par, N):
                upto(pe, N.xn_ready, b)
                if N is FN:
                    before(pe, acc_ready, b, NE)
                elif N is A0.norm:
                    before(pe, A0.x_done, b)
                else:
                    before(pe, qt_done, b)
                for c in range(KC):
                    i = t.transpose(N.bank[:, c * S:(c + 1) * S], N.xn[:, c * P:(c + 1) * P], ident)
                i.then_inc(N.xt_ready, 1)

            def qk(b, par, A):
                upto(pe, A.norm.xt_done, b)
                pe.wait_ge(A.ctx_in[par], dma_nth(b, par))
                before(pe, A0.o_ready if A.which == 0 else qy_ready, b)
                for j, src in enumerate((A.norm.xt, A.ctx[par])):
                    for c in range(KC):
                        for k in range(KC):
                            i = t.matmul(A.X[:, j * D + c * S:j * D + (c + 1) * S],
                                         wslice(A.w + j * KC * D, k, c * P, P, D), src[:, k, :],
                                         start=(k == 0), stop=(k == KC - 1))
                i.then_inc(A.qk_ready, 1)

            def vproj(b, par, A):
                pe.wait_ge(A.ctx_in[par], dma_nth(b, par))
                before(pe, A.ot_done, b)
                for k in range(KC):
                    i = t.matmul(A.Y[:, 0:D], A.ctx[par][:, k, :], wslice(A.w + 2 * KC * D, k, 0, D, D),
                                 start=(k == 0), stop=(k == KC - 1))
                i.then_inc(A.v_ready, 1)

            def scores(b, par, A, u):
                if u == 0:
                    upto(pe, A.k_done, b)
                if u == 1:
                    upto(pe, A.v_done, b)
                if u >= 2:
                    upto(pe, A.t_ready, b, NU, u - 1)
                for g in range(2):
                    r = 2 * HD * u
                    i = t.matmul(A.bank(u)[:, g * 2 * S:(g + 1) * 2 * S], A.q[r:r + 2 * HD, g, :],
                                 A.k[r:r + 2 * HD, g, :, :], start=True, stop=True)
                i.then_inc(A.s_ready, 1)

            def weights_t(b, par, A, u):
                upto(pe, A.p_ready, b, NU, u + 1)
                if u > 0:
                    upto(pe, A.pt_done, b, NU, u)
                for j in range(UH):
                    i = t.transpose(A.Z[:, j * S:(j + 1) * S], A.p[:, u, j, :], ident)
                i.then_inc(A.pt_ready, 1)

            def weighted(b, par, A, u):
                upto(pe, A.pt_done, b, NU, u + 1)
                if u == 0:
                    upto(pe, A.t_ready, b, NU, 3)
                for j in range(UH):
                    hh = j // 2 * (H // KC) + 2 * u + j % 2
                    i = t.matmul(A.X[:, hh * (HD + 1):(hh + 1) * (HD + 1)], A.pt[:, u, j, :], A.v[:, hh, :],
                                 start=True, stop=True)
                i.then_inc(A.av_ready, 1)

            def out_t(b, par, A):
                upto(pe, A.o_ready, b)
                o = A.o[:, :, :].rearrange("p h d -> p (h d)")
                for c in range(KC):
                    i = t.transpose(A.Y[:, c * S:(c + 1) * S], o[:, c * P:(c + 1) * P], ident)
                i.then_inc(A.ot_ready, 1)

            def out_proj(b, par, A):
                upto(pe, A.ot_done, b)
                for k in range(KC):
                    i = t.matmul(A.Z[:, 0:D], A.ot[:, k, :], wslice(A.w + 3 * KC * D, k, 0, D, D),
                                 start=(k == 0), stop=(k == KC - 1))
                i.then_inc(A.y_ready, 1)

            def logits(b, par):
                upto(pe, FN.xt_done, b)
                before(pe, acc_ready, b, NE)
                for k in range(KC):
                    i = t.matmul(F1[:, 0:E], FN.xt[:, k, :], csl("rw", k * E, E), start=(k == 0), stop=(k == KC - 1))
                i.then_inc(lgm_ready, 1)

            def gates_t(b, par):
                upto(pe, cf_ready, b)
                upto(pe, lg_ready, b)
                t.transpose(F1[0:NE, 0:S], cf9[:, :], ident).then_inc(cft_ready, 1)

            def hidden(b, par, i):
                if i == 0:
                    upto(pe, FN.xt_done, b)
                if i == 1:
                    upto(pe, cft_done, b)
                if i == 2:
                    upto(pe, h_ready, b, len(HU), 1)
                lo, hi = HU[i]
                for e in range(lo, hi):
                    o = (F0, F1)[i % 2][:, (e - lo) * S:(e - lo + 1) * S]
                    off = 2 * ATT_W + e * KC * HID
                    for k in range(KC):
                        n = t.matmul(o, wslice(off, k, 0, HID, HID), FN.xt[:, k, :], start=(k == 0),
                                     stop=(k == KC - 1))
                n.then_inc(hm_ready, 1)

            def expert(bank, e, half_, first):
                return t.matmul(bank[:, half_ * D:(half_ + 1) * D], h[:, e, :],
                                wslice(2 * ATT_W + W1_W, e, 0, D, D), start=first, stop=True)

            def shared_out(b, par):
                upto(pe, h_ready, b, len(HU), 2)
                t.matmul(F1[:, 0:D], cfT[:, :], b2_sb[:, :], start=True, stop=False)
                expert(F1, 0, 0, False).then_inc(ym_ready, 1)

            def pair_out(b, par, j):
                if j == 0:
                    upto(pe, h_ready, b, len(HU))
                if j == 1:
                    upto(pe, acc_ready, b, NE, 1)
                if j >= 2:
                    upto(pe, acc_ready, b, NE, 2 * (j - 2) + 3)
                bank = (F0, F1)[j % 2]
                expert(bank, 1 + 2 * j, 0, True)
                expert(bank, 2 + 2 * j, 1, True).then_inc(ym_ready, 1)

            def q_t(b, par):
                upto(pe, qb_ready, b)
                for c in range(KC):
                    i = t.transpose(A1.Z[:, c * (S // 2):(c + 1) * (S // 2)].bitcast(BF16), qb[:, c * P:(c + 1) * P],
                                    ident_b[:, :])
                i.then_inc(qt_ready, 1)

            def q_mm(b, par):
                upto(pe, qt_done, b)
                for k in range(KC):
                    i = t.matmul(A1.X[:, 0:D], qT[:, k, :], rhs_q[:, k, :], start=(k == 0), stop=(k == KC - 1))
                i.then_inc(qm_ready, 1)

            def step(s, par):
                at(s, par, 1, norm_t, A0.norm)
                at(s, par, 1, qk, A0)
                at(s, par, 3, vproj, A1)
                at(s, par, 1, vproj, A0)
                at(s, par, 4, q_t)
                at(s, par, 4, q_mm)
                at(s, par, 3, norm_t, A1.norm)
                at(s, par, 1, scores, A0, 0)
                at(s, par, 3, qk, A1)
                at(s, par, 2, norm_t, FN)
                at(s, par, 1, scores, A0, 1)
                at(s, par, 2, logits)
                at(s, par, 1, scores, A0, 2)
                at(s, par, 3, scores, A1, 0)
                at(s, par, 3, scores, A1, 1)
                at(s, par, 2, hidden, 0)
                at(s, par, 3, scores, A1, 2)
                at(s, par, 1, weights_t, A0, 0)
                at(s, par, 1, scores, A0, 3)
                at(s, par, 3, scores, A1, 3)
                at(s, par, 3, weights_t, A1, 0)
                at(s, par, 1, weighted, A0, 0)
                at(s, par, 3, weights_t, A1, 1)
                at(s, par, 1, weights_t, A0, 1)
                at(s, par, 3, weighted, A1, 0)
                at(s, par, 1, weights_t, A0, 2)
                at(s, par, 2, gates_t)
                at(s, par, 3, weights_t, A1, 2)
                at(s, par, 3, weighted, A1, 1)
                at(s, par, 1, weighted, A0, 1)
                at(s, par, 2, hidden, 1)
                at(s, par, 3, weights_t, A1, 3)
                at(s, par, 1, weighted, A0, 2)
                at(s, par, 3, weighted, A1, 2)
                at(s, par, 1, weights_t, A0, 3)
                at(s, par, 2, hidden, 2)
                at(s, par, 2, shared_out)
                at(s, par, 1, weighted, A0, 3)
                at(s, par, 2, pair_out, 0)
                at(s, par, 2, pair_out, 1)
                at(s, par, 3, weighted, A1, 3)
                at(s, par, 1, out_t, A0)
                at(s, par, 2, pair_out, 2)
                at(s, par, 2, pair_out, 3)
                at(s, par, 3, out_t, A1)
                at(s, par, 1, out_proj, A0)
                at(s, par, 3, out_proj, A1)

            run(pe, step)


_INS = ("x", "ctxT", "mask", "weights", "cols", "rows", "b2", "rel", "rhsT")


def lay_out(i):
    import numpy as np

    def a(n):
        return np.ascontiguousarray(i[n])

    def chunks(w):
        return w.reshape(-1, P, w.shape[-1]).transpose(1, 0, 2).reshape(P, -1)

    att = [chunks(a(f"L{layer}_xattn_{n}").T) for layer, names in ((0, ("Wq", "Wk", "Wv", "Wo")),
                                                                  (1, ("w_q", "w_k", "w_v", "w_o"))) for n in names]
    w1 = [chunks(a("L0_ffn_sW1"))] + [chunks(w) for w in a("L0_ffn_rW1")]
    w2 = [a("L0_ffn_sW2")] + list(a("L0_ffn_rW2"))
    weights = np.concatenate(att + w1 + w2, axis=1)
    r = np.arange(P)
    f = np.float32
    q, key = r[:, None], r[None, :]
    inside = (key - q + W - 1 >= 0) & (key <= q) & (key - q + W - 1 <= q)
    pads = np.where(r < W - 1, np.minimum(r, W - 2 - r) + 1, 0)
    cols = np.concatenate([
        a("L0_xattn_bq").reshape(KC, P).T, a("L0_xattn_bk").reshape(KC, P).T,
        np.concatenate([a("L0_ffn_sb1")[None], a("L0_ffn_rb1")]).T,
        chunks(a("L0_ffn_routing_W").T),
        (r // HD % 2 == 0).astype(f)[:, None], (r // HD % 2 == 1).astype(f)[:, None],
        np.where(r < W - 1, 0.0, HUGE).astype(f)[:, None], pads.astype(f)[:, None],
        np.eye(P, dtype=f), np.where(inside, 0.0, MASKED).astype(f), np.zeros((P, 6), f)], axis=1)
    rows = np.concatenate([a("L0_xattn_bv"), a("L0_xattn_bo"), a("L0_ffn_expert_bias"),
                           np.stack([a("g_xattn")[0], a("g_xattn")[1], a("g_ffn")[0], a("g_ffn")[1]])])
    b2 = np.concatenate([a("L0_ffn_rb2"), a("L0_ffn_sb2")[None]])
    ctxT = a("ctx_1024").reshape(B, S, KC, P).transpose(0, 3, 2, 1)
    at = r[:, None] - r[None, :] + a("L1_xattn_rel_emb").shape[0] // 2
    by_unit = np.arange(H).reshape(KC, NU, 2).transpose(1, 0, 2).reshape(-1)
    rel = a("L1_xattn_rel_emb")[at].transpose(0, 2, 1)[:, by_unit]
    rhsT = a("L1_ffn_rhs").T.reshape(KC, P, D).transpose(1, 0, 2)
    mask = a("mask_Bx1xSxS2_bf1").reshape(B, S, S).view(np.uint8)
    return {"x": a("x"), "ctxT": ctxT, "mask": mask, "weights": weights, "cols": cols, "rows": rows, "b2": b2,
            "rel": rel, "rhsT": rhsT}


def kernel(**inputs):
    import numpy as _np
    import concourse.bacc as _bacc
    from concourse import mybir as _mybir
    from concourse.bass_utils import run_bass_kernel_spmd as _run

    nc = _bacc.Bacc("TRN2", target_bir_lowering=False, num_devices=1)
    arrays, args = {}, []
    laid = lay_out(inputs)
    for name in _INS:
        v = _np.ascontiguousarray(laid[name])
        arrays[f"in_{name}_dram"] = v
        args.append(nc.dram_tensor(f"in_{name}_dram", v.shape, _mybir.dt.from_np(v.dtype), kind="ExternalInput").ap())
    args.append(nc.dram_tensor("out_0_dram", (B, S, D), _mybir.dt.float32, kind="ExternalOutput").ap())
    build(nc, *args)
    r = _run(nc, [arrays], core_ids=[0])
    return r.results[0]["out_0_dram"]
```

```python
from contextlib import ExitStack

import concourse.bass as bass
from concourse import mybir

P = 128
F32 = mybir.dt.float32
BF16 = mybir.dt.bfloat16
F16 = mybir.dt.float16
U8 = mybir.dt.uint8
ALU = mybir.AluOpType
ACT = mybir.ActivationFunctionType
AX_X = mybir.AxisListType.X

B, S, D = 16, 128, 256
H = 16
HD = D // H
W = 16
KC = D // P
HC = H // KC
E = 8
HID = 128
EPS = 1e-5
SCALE = HD ** -0.5
MASKED = -float(2 ** 100)
HUGE = 3.0e38
WSCALE = float(2 ** 15)
ROUND = 1.5 * 2 ** 23
UH = 4
NU = H // UH
VW = 1 + 3 * HD
UW = UH * S

ATT_W = 4 * KC * D
NE = E + 1
W1_W = NE * KC * HID
W2_W = NE * D


def column_consts():
    at, n = {}, 0
    for name, w in (("bq", KC), ("bk", KC), ("b1", NE), ("rw", KC * E), ("even", 1), ("odd", 1),
                    ("ncap", 1), ("npad", 1), ("ident", P), ("band", S), ("minus", 6)):
        at[name] = slice(n, n + w)
        n += w
    return at, n


COL, NCOL = column_consts()


def row_consts():
    at, n = {}, 0
    for name, w in (("bv", D), ("bo", D), ("eb", E), ("g", 4)):
        at[name] = slice(n, n + w)
        n += w
    return at, n


ROW, NROW = row_consts()
LAG = 5
PROLOGUE, STEPS = (LAG + 3) // 2 * 2, B + LAG


def build(nc, x, ctxT, mask, weights, cols, rows, b2, rel, rhsT, out):
    with ExitStack() as ctx:
        def sb(name, shape, dt=F32):
            return ctx.enter_context(nc.sbuf_tensor(name, shape, dt))

        def ps(name, shape=(P, 512), dt=F32):
            return ctx.enter_context(nc.psum_tensor(name, list(shape), dt))

        def sem(name):
            return ctx.enter_context(nc.semaphore(name))

        NW = 2 * ATT_W + W1_W + W2_W
        w_sb = sb("w_sb", [P, NW])
        col = sb("col", [P, NCOL])
        row = sb("row", [P, NROW])
        b2_sb = sb("b2_sb", [NE, D])
        rel_sb = sb("rel_sb", [P, H, S])
        bqs = sb("bqs", [P, KC])
        bkm = sb("bkm", [P, 2, KC])
        gate = sb("gate", [P, 4])
        gbo = sb("gbo", [P, D])
        half = sb("half", [P, E])
        minus_half = sb("minus_half", [P, 1])
        ident_b = sb("ident_b", [P, P], BF16)
        rhs_raw = sb("rhs_raw", [P, KC, D])
        rhs_am = sb("rhs_am", [P, 4 * KC])
        rhs_qT = sb("rhs_qT", [P, KC, D])
        rhs_q = sb("rhs_q", [P, KC, D], BF16)
        rhs_sc = sb("rhs_sc", [P, D])
        ident = col[:, COL["ident"]]
        band = col[:, COL["band"]]

        def csl(name, i=0, n=1):
            a = COL[name].start + i
            return col[:, a:a + n]

        class Norm:
            def __init__(self, n, bank):
                self.stat = sb(f"{n}_stat", [P, 6])
                self.mv = sb(f"{n}_mv", [P, 2])
                self.ve = sb(f"{n}_ve", [P, 1])
                self.rstd = sb(f"{n}_rstd", [P, 1])
                self.xn = sb(f"{n}_xn", [P, D])
                self.xt = sb(f"{n}_xt", [P, KC, S])
                self.bank = bank
                self.stat_ready = sem(f"{n}_stat_ready")
                self.mv_ready = sem(f"{n}_mv_ready")
                self.ve_ready = sem(f"{n}_ve_ready")
                self.rstd_ready = sem(f"{n}_rstd_ready")
                self.xn_ready = sem(f"{n}_xn_ready")
                self.xt_ready = sem(f"{n}_xt_ready")
                self.xt_done = sem(f"{n}_xt_done")

        class Attention:
            def __init__(self, n, which):
                self.which = which
                self.X, self.Y, self.Z = ps(f"{n}_X"), ps(f"{n}_Y"), ps(f"{n}_Z")
                self.norm = Norm(n, self.Z)
                self.w = which * ATT_W
                self.ctx = [sb(f"{n}_ctx{i}", [P, KC, S]) for i in range(2)]
                self.q = sb(f"{n}_q", [P, KC, S])
                self.k = sb(f"{n}_k", [P, KC, 2, S])
                self.v = sb(f"{n}_v", [P, H, HD])
                self.v_rest = sb(f"{n}_v_rest", [P, H, HD])
                self.v_parts = sb(f"{n}_v_parts", [P, H, VW], BF16)
                self.v_high, self.v_mid, self.v_low = (
                    self.v_parts[:, :, 1 + i * HD:1 + (i + 1) * HD] for i in range(3))
                self.sum = sb(f"{n}_sum", [P, H, HD])
                self.t = sb(f"{n}_t", [P, NU, UH, S])
                self.nm = sb(f"{n}_nm", [P, H])
                self.nmc = sb(f"{n}_nmc", [P, H]) if which == 0 else self.nm
                self.p = self.t
                self.pt_high = sb(f"{n}_pt_high", [P, NU, UH, S], F16)
                self.pt_low = sb(f"{n}_pt_low", [P, NU, UH, S], F16)
                self.e0a = sb(f"{n}_e0a", [P, H])
                self.e0 = sb(f"{n}_e0", [P, H])
                self.den = sb(f"{n}_den", [P, H])
                self.rden = sb(f"{n}_rden", [P, H])
                self.o = sb(f"{n}_o", [P, H, HD])
                self.ot = sb(f"{n}_ot", [P, KC, S])
                self.ctx_in = [sem(f"{n}_ctx_in{i}") for i in range(2)]
                for_each = ("qk_ready v_ready k_done v_done s_ready t_ready "
                            "sum_ready v_high_done v_rest_done v_mid_done v_low_done "
                            "nm_ready nmc_ready sub_done p_ready pt_ready pt_high_done pt_done av_ready "
                            "e0a_ready e0_ready "
                            "den_ready rden_ready o_ready ot_ready ot_done y_ready x_done").split()
                (self.qk_ready, self.v_ready, self.k_done,
                 self.v_done, self.s_ready, self.t_ready, self.sum_ready, self.v_high_done, self.v_rest_done,
                 self.v_mid_done, self.v_low_done, self.nm_ready, self.nmc_ready, self.sub_done,
                 self.p_ready, self.pt_ready, self.pt_high_done, self.pt_done, self.av_ready,
                 self.e0a_ready, self.e0_ready,
                 self.den_ready, self.rden_ready, self.o_ready, self.ot_ready, self.ot_done,
                 self.y_ready, self.x_done) = [sem(f"{n}_{k}") for k in for_each]
                if which == 0:
                    self.xb_ready = sem(f"{n}_xb_ready")

            def bank(self, u):
                return (self.X, self.Y)[u % 2]

        A0, A1 = Attention("a0", 0), Attention("a1", 1)

        x0 = [sb(f"x0_{i}", [P, D]) for i in range(2)]
        x0b = sb("x0b", [P, D])
        x1 = [sb(f"x1_{i}", [P, D]) for i in range(2)]
        x2 = [sb(f"x2_{i}", [P, D]) for i in range(2)]
        x3 = sb("x3", [P, D])
        y_sb = [sb(f"y_{i}", [P, D]) for i in range(2)]
        mask_u8 = [sb(f"mask_u8_{i}", [P, S], U8) for i in range(2)]
        mask_neg = sb("mask_neg", [P, S])
        bm = sb("bm", [P, H, S])

        F0, F1 = ps("F0"), ps("F1")
        FN = Norm("f", F0)
        lg, lab, lex, kept, lost, lln, lmax, lsp = (sb(n, [P, E]) for n in (
            "lg", "lab", "lex", "kept", "lost", "lln", "lmax", "lsp"))
        act14 = sb("act14", [P, E + 6])
        mx8 = sb("mx8", [P, 8])
        rep8 = sb("rep8", [P, 8])
        zap = sb("zap", [P, E + 6])
        cf9 = sb("cf9", [P, NE])
        cfg = sb("cfg", [P, E])
        cfT = sb("cfT", [NE, S])
        h = sb("h", [P, NE, S])
        acc = [sb(f"acc_{i}", [P, D]) for i in range(2)]
        HU = [(0, 4), (4, 8), (8, 9)]
        (lgm_ready, lg_ready, lab_ready, lex_ready, kept_ready, lost_ready, lln_ready, lmax_ready,
         lsp_ready, act_ready, mx_ready, rep_ready, zap_ready, cf_ready, cfg_ready,
         cft_ready, cft_done, hm_ready, h_ready, ym_ready,
         acc_ready) = [sem(n) for n in (
             "lgm_ready lg_ready lab_ready lex_ready kept_ready lost_ready lln_ready lmax_ready "
             "lsp_ready act_ready mx_ready rep_ready "
             "zap_ready cf_ready cfg_ready cft_ready cft_done hm_ready h_ready ym_ready "
             "acc_ready").split()]

        QN = Norm("q", None)
        am = sb("am", [P, 1])
        lsc = sb("lsc", [P, 1])
        rsc = sb("rsc", [P, 1])
        qf = sb("qf", [P, D])
        qc = sb("qc", [P, D])
        qb = sb("qb", [P, D], BF16)
        qT = sb("qT", [P, KC, S], BF16)
        qy = sb("qy", [P, D])
        (am_ready, lsc_ready, rsc_ready, qf_ready, qc_ready, qb_ready, qt_ready, qt_done, qm_ready, qy_ready,
         y_ready) = [sem(n) for n in (
             "am_ready lsc_ready rsc_ready qf_ready qc_ready qb_ready qt_ready qt_done qm_ready qy_ready "
             "y_ready").split()]

        x_in = [sem(f"x_in{i}") for i in range(2)]
        mask_in = [sem(f"mask_in{i}") for i in range(2)]
        y_out = [sem(f"y_out{i}") for i in range(2)]
        mneg_ready, bm_ready = sem("mneg_ready"), sem("bm_ready")
        c_in, r_in, gtanh = sem("c_in"), sem("r_in"), sem("gtanh")
        w0_in, wf_in, w1_in, b2_in, rel_in = (sem(n) for n in ("w0_in", "wf_in", "w1_in", "b2_in", "rel_in"))
        pool_set, act_set, dve_set = sem("pool_set"), sem("act_set"), sem("dve_set")
        r_t, r_q, r_s = sem("r_t"), sem("r_q"), sem("r_s")
        waits_apart = sem("waits_apart")


        def upto(eng, s, b, per=1, k=None):
            eng.wait_ge(s, b * per + (per if k is None else k))

        def before(eng, s, b, per=1, k=None):
            n = b * per + (per if k is None else k) - per
            if type(n) is not int or n > 0:
                eng.wait_ge(s, n)

        def before2(eng, s, b, per=1, k=None):
            n = b * per + (per if k is None else k) - 2 * per
            if type(n) is not int or n > 0:
                eng.wait_ge(s, n)

        def at_first(eng, s, b):
            if type(b) is int and b == 0:
                eng.wait_ge(s, 16)

        def dma_nth(b, par):
            return (b - par) * 8 + 16

        def settled(eng):
            eng.wait_ge(pool_set, 7)
            eng.wait_ge(act_set, 3)
            eng.wait_ge(dve_set, 2)

        def apart(eng):
            eng.sem_inc(waits_apart, 1)

        def unit_heads(t, u):
            return t[:, :].rearrange("p (c u j) -> p c u j", c=KC, u=NU)[:, :, u, :]

        def run(eng, step):
            for s in range(PROLOGUE):
                step(s, s % 2)
            with eng.Fori(PROLOGUE // 2, B // 2, 1) as turn_:
                step(turn_ * 2, 0)
                step(turn_ * 2 + 1, 1)
            for s in range(B, STEPS):
                step(s, s % 2)

        def at(s, par, lag, part, *what):
            if type(s) is not int or 0 <= s - lag < B:
                part(s - lag, (par + lag) % 2, *what)

        def wslice(off, k, m0, m, width):
            a = off + k * width + m0
            return w_sb[:, a:a + m]

        block = ctx.enter_context(nc.Block())

        @block.sync
        def _(sp):
            sp.dma_start(col[:, :], cols).then_inc(c_in, 16)
            sp.dma_start(row[:, :], rows.partition_broadcast(P)).then_inc(c_in, 16)
            sp.dma_start(rhs_raw[:, :, :], rhsT).then_inc(r_in, 16)
            sp.dma_start(w_sb[:, 0:ATT_W], weights[:, 0:ATT_W]).then_inc(w0_in, 16)

            def later_constants():
                sp.dma_start(w_sb[:, 2 * ATT_W:NW], weights[:, 2 * ATT_W:NW]).then_inc(wf_in, 16)
                sp.dma_start(b2_sb[:, :], b2).then_inc(b2_in, 16)
                sp.dma_start(rel_sb[:, :, :], rel).then_inc(rel_in, 16)
                sp.dma_start(w_sb[:, ATT_W:2 * ATT_W], weights[:, ATT_W:2 * ATT_W]).then_inc(w1_in, 16)

            def load_x(b, par):
                before2(sp, A0.xb_ready, b)
                before2(sp, A0.norm.xn_ready, b)
                apart(sp)
                sp.dma_start(x0[par][:, :], x[b]).then_inc(x_in[par], 16)

            def load_ctx(b, par, A):
                before2(sp, A.v_ready, b)
                before2(sp, A.qk_ready, b)
                apart(sp)
                sp.dma_start(A.ctx[par][:, :, :], ctxT[b]).then_inc(A.ctx_in[par], 16)

            def load_mask(b, par):
                before2(sp, mneg_ready, b)
                apart(sp)
                sp.dma_start(mask_u8[par][:, :], mask[b]).then_inc(mask_in[par], 16)

            def store(b, par):
                upto(sp, y_ready, b)
                apart(sp)
                sp.dma_start(out[b], y_sb[par][:, :]).then_inc(y_out[par], 16)

            def step(s, par):
                at(s, par, 1, load_x)
                at(s, par, 0, load_ctx, A0)
                at(s, par, 3, load_mask)
                at(s, par, 5, store)
                at(s, par, 3, load_ctx, A1)
                if type(s) is int and s == 1:
                    later_constants()

            run(sp, step)
            for i in range(2):
                sp.wait_ge(y_out[i], 16 * (B // 2))

        @block.gpsimd
        def _(pool):
            g = nc.gpsimd
            pool.wait_ge(c_in, 32)
            g.memset(half[:, :], 0.5).then_inc(pool_set, 1)
            g.memset(minus_half[:, :], -0.5).then_inc(pool_set, 1)
            g.memset(A0.v_parts[:, :, 0:1], 1.0).then_inc(pool_set, 1)
            g.memset(A1.v_parts[:, :, 0:1], 1.0).then_inc(pool_set, 1)
            g.memset(rep8[:, :], -1.0).then_inc(pool_set, 1)
            g.memset(cf9[:, :], 1.0).then_inc(pool_set, 1)
            g.memset(act14[:, :], -1.0).then_inc(pool_set, 1)

            def rstd(b, par, N):
                upto(pool, N.mv_ready, b)
                apart(pool)
                g.tensor_scalar(N.ve[:, :], N.mv[:, 1:2], EPS, None, ALU.add).then_inc(N.ve_ready, 1)
                upto(pool, N.ve_ready, b)
                g.tensor_tensor(N.rstd[:, :], N.ve[:, :], minus_half[:, :], ALU.pow).then_inc(N.rstd_ready, 1)

            def add_bo(b, par):
                pool.wait_ge(x_in[par], dma_nth(b, par))
                before(pool, A0.x_done, b)
                g.tensor_tensor(x0b[:, :], x0[par][:, :], gbo[:, :], ALU.add).then_inc(A0.xb_ready, 1)

            def bias_mask(b, par):
                at_first(pool, rel_in, b)
                pool.wait_ge(mask_in[par], dma_nth(b, par))
                apart(pool)
                g.tensor_scalar(mask_neg[:, :], mask_u8[par][:, :], 0.0, MASKED, ALU.is_equal,
                                ALU.mult).then_inc(mneg_ready, 1)
                upto(pool, mneg_ready, b)
                for u in range(NU):
                    before(pool, A1.t_ready, b, NU, u + 1)
                    g.tensor_tensor(bm[:, UH * u:UH * (u + 1), :], rel_sb[:, UH * u:UH * (u + 1), :],
                                    mask_neg[:, None, :].to_broadcast([P, UH, S]),
                                    ALU.add).then_inc(bm_ready, 1)

            def subtract(b, par, A, u):
                upto(pool, A.nm_ready, b, NU, u + 1)
                if A.which == 0:
                    apart(pool)
                    g.tensor_scalar(unit_heads(A.nmc, u), unit_heads(A.nm, u), csl("ncap"), None,
                                    ALU.min).then_inc(A.nmc_ready, 1)
                    upto(pool, A.nmc_ready, b, NU, u + 1)
                t4 = A.t[:, u, :, :].rearrange("p (c j) t -> p c j t", c=KC)
                g.tensor_tensor(t4, t4, unit_heads(A.nmc, u)[:, :, :, None].to_broadcast([P, KC, 2, S]),
                                ALU.add).then_inc(A.sub_done, 1)

            def v_rest(b, par, A):
                upto(pool, A.v_high_done, b)
                g.tensor_tensor(A.v_rest[:, :, :], A.v[:, :, :], A.v_high,
                                ALU.subtract).then_inc(A.v_rest_done, 1)

            def v_low(b, par, A):
                upto(pool, A.v_mid_done, b)
                g.tensor_tensor(A.v_low, A.v_rest[:, :, :], A.v_mid,
                                ALU.subtract).then_inc(A.v_low_done, 1)

            def heads_scaled(b, par, A):
                upto(pool, A.rden_ready, b)
                g.tensor_tensor(A.o[:, :, :], A.sum[:, :, :], A.rden[:, :, None].to_broadcast([P, H, HD]),
                                ALU.mult).then_inc(A.o_ready, 1)

            def activation_root(b, par):
                upto(pool, lsp_ready, b)
                g.tensor_tensor(act14[:, 0:E], lsp[:, :], half[:, :], ALU.pow).then_inc(act_ready, 1)

            def step(s, par):
                at(s, par, 3, bias_mask)
                at(s, par, 4, heads_scaled, A1)
                at(s, par, 2, rstd, FN)
                at(s, par, 4, rstd, QN)
                at(s, par, 3, rstd, A1.norm)
                at(s, par, 1, v_rest, A0)
                at(s, par, 1, subtract, A0, 0)
                at(s, par, 1, subtract, A0, 1)
                at(s, par, 1, subtract, A0, 2)
                at(s, par, 1, subtract, A0, 3)
                at(s, par, 2, activation_root)
                at(s, par, 3, subtract, A1, 0)
                at(s, par, 3, v_rest, A1)
                at(s, par, 3, subtract, A1, 1)
                at(s, par, 1, v_low, A0)
                at(s, par, 3, subtract, A1, 2)
                at(s, par, 3, subtract, A1, 3)
                at(s, par, 1, add_bo)
                at(s, par, 0, rstd, A0.norm)
                at(s, par, 1, heads_scaled, A0)
                at(s, par, 3, v_low, A1)

            settled(pool)
            run(pool, step)

        @block.scalar
        def _(act):
            a = nc.scalar
            act.wait_ge(c_in, 32)
            a.activation(gate[:, :], row[:, ROW["g"]], ACT.Tanh).then_inc(gtanh, 1)
            a.activation(bqs[:, :], col[:, COL["bq"]], ACT.Copy, scale=SCALE).then_inc(act_set, 1)
            for j, m in enumerate(("even", "odd")):
                a.activation(bkm[:, j, :], col[:, COL["bk"]], ACT.Copy, scale=csl(m)).then_inc(act_set, 1)
            settled(act)

            def exp_and_log_table():
                a.preload_act_table_set("natural_log_exp_and_others")

            def xt_out(b, par, N):
                upto(act, N.xt_ready, b)
                a.activation(N.xt[:, :, :], N.bank[:, 0:D].rearrange("p (c t) -> p c t", c=KC),
                             ACT.Copy).then_inc(N.xt_done, 1)

            def q_out(b, par, A):
                upto(act, A.qk_ready, b)
                if A.which == 0:
                    for c in range(KC):
                        a.activation(A.q[:, c, :], A.X[:, c * S:(c + 1) * S], ACT.Identity,
                                     bias=bqs[:, c:c + 1], scale=SCALE)
                else:
                    a.activation(A.q[:, :, :], A.X[:, 0:D].rearrange("p (c t) -> p c t", c=KC), ACT.Copy,
                                 scale=SCALE)

            def k_out(b, par, A):
                upto(act, A.qk_ready, b)
                for j, m in enumerate(("even", "odd")):
                    if A.which == 0:
                        for c in range(KC):
                            i = a.activation(A.k[:, c, j, :], A.X[:, D + c * S:D + (c + 1) * S], ACT.Identity,
                                             bias=bkm[:, j, c:c + 1], scale=csl(m))
                    else:
                        i = a.activation(A.k[:, :, j, :], A.X[:, D:2 * D].rearrange("p (c t) -> p c t", c=KC),
                                         ACT.Copy, scale=csl(m))
                i.then_inc(A.k_done, 1)

            def v_out1(b, par):
                upto(act, A1.v_ready, b)
                a.activation(A1.v[:, :, :], A1.Y[:, 0:D].rearrange("p (h d) -> p h d", h=H),
                             ACT.Copy).then_inc(A1.v_done, 1)

            def v_high(b, par, A):
                upto(act, A.v_done, b)
                a.activation(A.v_high, A.v[:, :, :], ACT.Copy).then_inc(A.v_high_done, 1)

            def v_mid(b, par, A):
                upto(act, A.v_rest_done, b)
                a.activation(A.v_mid, A.v_rest[:, :, :], ACT.Copy).then_inc(A.v_mid_done, 1)

            def exps(b, par, A, u):
                upto(act, A.sub_done, b, NU, u + 1)
                a.activation(A.p[:, u, :, :], A.t[:, u, :, :], ACT.Exp).then_inc(A.p_ready, 1)

            def pt_out(b, par, A, u):
                upto(act, A.pt_ready, b, NU, u + 1)
                a.activation(A.pt_high[:, u, :, :], A.Z[:, :].rearrange("p (h t) -> p h t", h=UH),
                             ACT.Copy, scale=WSCALE).then_inc(A.pt_high_done, 1)

            def pad_weight(b, par):
                upto(act, A0.e0a_ready, b)
                a.activation(A0.e0[:, :], A0.e0a[:, :], ACT.Exp).then_inc(A0.e0_ready, 1)

            def ot_out(b, par, A):
                upto(act, A.ot_ready, b)
                a.activation(A.ot[:, :, :], A.Y[:, 0:D].rearrange("p (c t) -> p c t", c=KC),
                             ACT.Copy).then_inc(A.ot_done, 1)

            def softplus_log(b, par):
                upto(act, lab_ready, b)
                a.activation(lex[:, :], lab[:, :], ACT.Exp, scale=-1.0).then_inc(lex_ready, 1)
                upto(act, lex_ready, b)
                a.activation(lln[:, :], lex[:, :], ACT.Ln, bias=1.0).then_inc(lln_ready, 1)

            def cft_out(b, par):
                upto(act, cft_ready, b)
                a.activation(cfT[:, :], F1[0:NE, 0:S], ACT.Copy).then_inc(cft_done, 1)

            def silus(b, par, i):
                upto(act, hm_ready, b, len(HU), i + 1)
                lo, hi = HU[i]
                for e in range(lo, hi):
                    n = a.activation(h[:, e, :], (F0, F1)[i % 2][:, (e - lo) * S:(e - lo + 1) * S], ACT.Silu,
                                     bias=csl("b1", e))
                n.then_inc(h_ready, 1)

            def qt_out(b, par):
                upto(act, qt_ready, b)
                a.activation(qT[:, :, :], A1.Z[:, 0:D // 2].bitcast(BF16).rearrange("p (c t) -> p c t", c=KC),
                             ACT.Copy).then_inc(qt_done, 1)

            def step(s, par):
                at(s, par, 2, pt_out, A0, 3)
                at(s, par, 3, silus, 1)
                at(s, par, 3, silus, 2)
                at(s, par, 4, pt_out, A1, 1)
                exp_and_log_table()
                at(s, par, 4, exps, A1, 2)
                at(s, par, 4, pt_out, A1, 2)
                at(s, par, 4, exps, A1, 3)
                at(s, par, 4, pt_out, A1, 3)
                at(s, par, 2, ot_out, A0)
                at(s, par, 4, ot_out, A1)
                at(s, par, 1, xt_out, A0.norm)
                at(s, par, 1, q_out, A0)
                at(s, par, 2, xt_out, FN)
                at(s, par, 1, k_out, A0)
                at(s, par, 4, qt_out)
                at(s, par, 1, v_high, A0)
                at(s, par, 3, xt_out, A1.norm)
                at(s, par, 1, exps, A0, 0)
                at(s, par, 3, q_out, A1)
                at(s, par, 3, k_out, A1)
                at(s, par, 3, v_out1)
                at(s, par, 1, pt_out, A0, 0)
                at(s, par, 1, exps, A0, 1)
                at(s, par, 2, softplus_log)
                at(s, par, 1, exps, A0, 2)
                at(s, par, 1, pt_out, A0, 1)
                at(s, par, 3, v_high, A1)
                at(s, par, 1, exps, A0, 3)
                at(s, par, 1, v_mid, A0)
                at(s, par, 1, pad_weight)
                at(s, par, 3, exps, A1, 0)
                at(s, par, 3, v_mid, A1)
                at(s, par, 1, pt_out, A0, 2)
                at(s, par, 3, pt_out, A1, 0)
                at(s, par, 3, exps, A1, 1)
                at(s, par, 2, cft_out)
                at(s, par, 2, silus, 0)

            run(act, step)

        @block.vector
        def _(dve):
            v = nc.vector
            dve.wait_ge(c_in, 32)
            v.tensor_copy(ident_b[:, :], ident).then_inc(dve_set, 1)
            dve.wait_ge(gtanh, 1)
            v.tensor_scalar(gbo[:, :], row[:, ROW["bo"]], gate[:, 0:1], None, ALU.mult).then_inc(dve_set, 1)
            dve.wait_ge(r_in, 16)
            for c in range(KC):
                i = v.tensor_reduce(rhs_am[:, c:c + 1], rhs_raw[:, c, :], AX_X, ALU.max, apply_absolute_value=True)
            i.then_inc(r_s, 1)
            dve.wait_ge(r_s, 1)
            v.tensor_scalar(rhs_am[:, 2:4], rhs_am[:, 0:2], 1e-12, 1.0 / 127.0, ALU.max, ALU.mult).then_inc(r_s, 1)
            dve.wait_ge(r_s, 2)
            v.reciprocal(rhs_am[:, 4:6], rhs_am[:, 2:4]).then_inc(r_s, 1)
            dve.wait_ge(r_s, 3)
            for c in range(KC):
                i = v.tensor_scalar(rhs_qT[:, c, :], rhs_raw[:, c, :], rhs_am[:, 4 + c:5 + c], ROUND,
                                    ALU.mult, ALU.add)
            i.then_inc(r_q, 1)
            dve.wait_ge(r_q, 1)
            v.tensor_scalar(rhs_qT[:, :, :], rhs_qT[:, :, :], ROUND + 127.0, ROUND - 127.0, ALU.min,
                            ALU.max).then_inc(r_q, 1)
            dve.wait_ge(r_q, 2)
            v.tensor_scalar(rhs_qT[:, :, :], rhs_qT[:, :, :], ROUND, None, ALU.subtract).then_inc(r_q, 1)
            dve.wait_ge(r_t, 1)
            v.tensor_copy(rhs_q[:, :, :], A0.X[:, :].rearrange("p (k n) -> p k n", k=KC)).then_inc(r_q, 1)
            v.tensor_copy(rhs_sc[:, :], A0.Y[:, 0:D]).then_inc(r_q, 1)
            settled(dve)

            def source(b, par, N):
                if N is A0.norm:
                    return x0[par], x_in[par], dma_nth(b, par)
                if N is FN:
                    return x1[par], A0.x_done, b + 1
                if N is A1.norm:
                    return x2[par], acc_ready, b * NE + NE
                return x3, A1.x_done, b + 1

            def stats(b, par, N):
                src, ready, n = source(b, par, N)
                dve.wait_ge(ready, n)
                v.bn_stats(N.stat[:, :], src[:, :]).then_inc(N.stat_ready, 1)
                upto(dve, N.stat_ready, b)
                apart(dve)
                v.bn_aggr(N.mv[:, :], N.stat[:, :]).then_inc(N.mv_ready, 1)

            def normalise(b, par, N):
                upto(dve, N.rstd_ready, b)
                if N.bank is not None:
                    before(dve, N.xt_ready, b)
                v.tensor_scalar(N.xn[:, :], source(b, par, N)[0][:, :], N.mv[:, 0:1], N.rstd[:, 0:1], ALU.subtract,
                                ALU.mult).then_inc(N.xn_ready, 1)

            def v_out0(b, par):
                upto(dve, A0.v_ready, b)
                v.tensor_tensor(A0.v[:, :, :], A0.Y[:, 0:D].rearrange("p (h d) -> p h d", h=H),
                                row[:, ROW["bv"]].rearrange("p (h d) -> p h d", h=H),
                                ALU.add).then_inc(A0.v_done, 1)

            def maxima(b, par, A, u):
                upto(dve, A.s_ready, b, NU, u + 1)
                if A.which == 0:
                    add = band[:, None, :].to_broadcast([P, UH, S])
                else:
                    upto(dve, bm_ready, b, NU, u + 1)
                    add = bm[:, UH * u:UH * (u + 1), :]
                v.tensor_tensor(A.t[:, u, :, :], A.bank(u)[:, :].rearrange("p (h t) -> p h t", h=UH), add,
                                ALU.add).then_inc(A.t_ready, 1)
                upto(dve, A.t_ready, b, NU, u + 1)
                v.tensor_reduce(unit_heads(A.nm, u), A.t[:, u, :, :].rearrange("p (c j) t -> p c j t", c=KC),
                                AX_X, ALU.max, negate=True).then_inc(A.nm_ready, 1)

            def pt_low(b, par, A, u):
                upto(dve, A.pt_high_done, b, NU, u + 1)
                v.scalar_tensor_tensor(out=A.pt_low[:, u, :, :].rearrange("p h t -> p (h t)"), in0=A.Z[:, :],
                                       scalar=WSCALE, in1=A.pt_high[:, u, :, :].rearrange("p h t -> p (h t)"),
                                       op0=ALU.mult, op1=ALU.subtract).then_inc(A.pt_done, 1)

            def pad_argument(b, par):
                upto(dve, A0.nmc_ready, b, NU)
                v.tensor_scalar(A0.e0a[:, :], A0.nmc[:, :], 0.0, None, ALU.min).then_inc(A0.e0a_ready, 1)

            def heads_out(b, par, A):
                upto(dve, A.av_ready, b, NU)
                ones = [bank[:, 0:HC * VW].rearrange("p (h d) -> p h d", h=HC)[:, :, 0] for bank in (A.X, A.Y)]
                if A.which == 0:
                    upto(dve, A.e0_ready, b)
                    for c in range(KC):
                        i = v.scalar_tensor_tensor(out=A.den[:, c * HC:(c + 1) * HC], in0=A.e0[:, c * HC:(c + 1) * HC],
                                                   scalar=csl("npad"), in1=ones[c], op0=ALU.mult, op1=ALU.add)
                    i.then_inc(A.den_ready, 1)
                for c, bank in enumerate((A.X, A.Y)):
                    parts = bank[:, 0:HC * VW].rearrange("p (h d) -> p h d", h=HC)[:, :, 1:VW]
                    i = v.tensor_reduce(A.sum[:, c * HC:(c + 1) * HC, :],
                                        parts.rearrange("p h (i d) -> p h d i", i=3), AX_X, ALU.add)
                i.then_inc(A.sum_ready, 1)
                if A.which == 0:
                    upto(dve, A.den_ready, b)
                    v.reciprocal(A.rden[:, :], A.den[:, :]).then_inc(A.rden_ready, 1)
                else:
                    for c in range(KC):
                        i = v.reciprocal(A.rden[:, c * HC:(c + 1) * HC], ones[c])
                    i.then_inc(A.rden_ready, 1)

            def residual0(b, par):
                upto(dve, A0.y_ready, b)
                upto(dve, A0.xb_ready, b)
                before2(dve, acc_ready, b, NE)
                v.scalar_tensor_tensor(out=x1[par][:, :], in0=A0.Z[:, 0:D], scalar=gate[:, 0:1], in1=x0b[:, :],
                                       op0=ALU.mult, op1=ALU.add).then_inc(A0.x_done, 1)

            def residual1(b, par):
                upto(dve, A1.y_ready, b)
                v.scalar_tensor_tensor(out=x3[:, :], in0=A1.Z[:, 0:D], scalar=gate[:, 1:2], in1=x2[par][:, :],
                                       op0=ALU.mult, op1=ALU.add).then_inc(A1.x_done, 1)

            def router(b, par):
                upto(dve, lgm_ready, b)
                v.tensor_tensor(lg[:, :], F1[:, 0:E], row[:, ROW["eb"]], ALU.add).then_inc(lg_ready, 1)
                upto(dve, lg_ready, b)
                v.scalar_tensor_tensor(out=lab[:, :], in0=lg[:, :], scalar=-1.0, in1=lg[:, :], op0=ALU.mult,
                                       op1=ALU.max).then_inc(lab_ready, 1)

            def softplus(b, par):
                upto(dve, lex_ready, b)
                v.tensor_scalar(kept[:, :], lex[:, :], 1.0, 1.0, ALU.add, ALU.subtract).then_inc(kept_ready, 1)
                upto(dve, kept_ready, b)
                v.tensor_tensor(lost[:, :], lex[:, :], kept[:, :], ALU.subtract).then_inc(lost_ready, 1)
                upto(dve, lln_ready, b)
                v.scalar_tensor_tensor(out=lmax[:, :], in0=lg[:, :], scalar=0.0, in1=lln[:, :], op0=ALU.max,
                                       op1=ALU.add).then_inc(lmax_ready, 1)
                upto(dve, lmax_ready, b)
                v.tensor_tensor(lsp[:, :], lmax[:, :], lost[:, :], ALU.add).then_inc(lsp_ready, 1)

            def top_two(b, par):
                upto(dve, act_ready, b)
                apart(dve)
                v.max(mx8[:, :], act14[:, 0:E]).then_inc(mx_ready, 1)
                upto(dve, mx_ready, b)
                v.tensor_copy(rep8[:, 0:2], mx8[:, 0:2]).then_inc(rep_ready, 1)
                upto(dve, rep_ready, b)
                apart(dve)
                v.match_replace(zap[:, :], rep8[:, :], act14[:, :], 0.0).then_inc(zap_ready, 1)
                upto(dve, zap_ready, b)
                v.tensor_tensor(cf9[:, 0:E], act14[:, 0:E], zap[:, 0:E], ALU.subtract).then_inc(cf_ready, 1)
                upto(dve, cf_ready, b)
                v.tensor_scalar(cfg[:, :], cf9[:, 0:E], gate[:, 2:3], None, ALU.mult).then_inc(cfg_ready, 1)

            def add_shared(b, par):
                upto(dve, ym_ready, b, 5, 1)
                v.scalar_tensor_tensor(out=acc[0][:, :], in0=F1[:, 0:D], scalar=gate[:, 2:3], in1=x1[par][:, :],
                                       op0=ALU.mult, op1=ALU.add).then_inc(acc_ready, 1)

            def add_pair(b, par, j):
                upto(dve, ym_ready, b, 5, 2 + j)
                bank = (F0, F1)[j % 2]
                for e in (2 * j, 2 * j + 1):
                    upto(dve, acc_ready, b, NE, e + 1)
                    if e == E - 1:
                        before2(dve, A1.x_done, b)
                    v.scalar_tensor_tensor(out=x2[par][:, :] if e == E - 1 else acc[(e + 1) % 2][:, :],
                                           in0=bank[:, (e % 2) * D:(e % 2 + 1) * D], scalar=cfg[:, e:e + 1],
                                           in1=acc[e % 2][:, :], op0=ALU.mult, op1=ALU.add).then_inc(acc_ready, 1)

            def quantise(b, par):
                upto(dve, QN.xn_ready, b)
                v.tensor_reduce(am[:, :], QN.xn[:, :], AX_X, ALU.max, apply_absolute_value=True).then_inc(am_ready, 1)
                upto(dve, am_ready, b)
                v.tensor_scalar(lsc[:, :], am[:, :], 1e-12, 1.0 / 127.0, ALU.max, ALU.mult).then_inc(lsc_ready, 1)
                upto(dve, lsc_ready, b)
                v.reciprocal(rsc[:, :], lsc[:, :]).then_inc(rsc_ready, 1)
                upto(dve, rsc_ready, b)
                v.tensor_scalar(qf[:, :], QN.xn[:, :], rsc[:, 0:1], ROUND, ALU.mult, ALU.add).then_inc(qf_ready, 1)
                upto(dve, qf_ready, b)
                v.tensor_scalar(qc[:, :], qf[:, :], ROUND + 127.0, ROUND - 127.0, ALU.min,
                                ALU.max).then_inc(qc_ready, 1)
                upto(dve, qc_ready, b)
                v.tensor_scalar(qb[:, :], qc[:, :], ROUND, None, ALU.subtract).then_inc(qb_ready, 1)

            def final(b, par):
                upto(dve, qm_ready, b)
                v.scalar_tensor_tensor(out=qy[:, :], in0=A1.X[:, 0:D], scalar=lsc[:, 0:1], in1=rhs_sc[:, :],
                                       op0=ALU.mult, op1=ALU.mult).then_inc(qy_ready, 1)
                upto(dve, qy_ready, b)
                n = dma_nth(b, par) - 16
                if type(n) is not int or n > 0:
                    dve.wait_ge(y_out[par], n)
                v.scalar_tensor_tensor(out=y_sb[par][:, :], in0=qy[:, :], scalar=gate[:, 3:4], in1=x3[:, :],
                                       op0=ALU.mult, op1=ALU.add).then_inc(y_ready, 1)

            def step(s, par):
                at(s, par, 2, heads_out, A0)
                at(s, par, 4, pt_low, A1, 1)
                at(s, par, 3, add_shared)
                at(s, par, 3, add_pair, 0)
                at(s, par, 4, pt_low, A1, 2)
                at(s, par, 3, add_pair, 1)
                at(s, par, 4, pt_low, A1, 3)
                at(s, par, 1, normalise, A0.norm)
                at(s, par, 4, heads_out, A1)
                at(s, par, 3, add_pair, 2)
                at(s, par, 2, residual0)
                at(s, par, 3, add_pair, 3)
                at(s, par, 2, stats, FN)
                at(s, par, 4, residual1)
                at(s, par, 4, stats, QN)
                at(s, par, 2, normalise, FN)
                at(s, par, 3, stats, A1.norm)
                at(s, par, 4, normalise, QN)
                at(s, par, 4, quantise)
                at(s, par, 1, v_out0)
                at(s, par, 3, normalise, A1.norm)
                at(s, par, 1, maxima, A0, 0)
                at(s, par, 4, final)
                at(s, par, 1, maxima, A0, 1)
                at(s, par, 1, maxima, A0, 2)
                at(s, par, 1, maxima, A0, 3)
                at(s, par, 2, router)
                at(s, par, 1, pt_low, A0, 0)
                at(s, par, 2, softplus)
                at(s, par, 3, maxima, A1, 0)
                at(s, par, 1, pt_low, A0, 1)
                at(s, par, 1, pad_argument)
                at(s, par, 3, maxima, A1, 1)
                at(s, par, 2, top_two)
                at(s, par, 1, pt_low, A0, 2)
                at(s, par, 3, maxima, A1, 2)
                at(s, par, 3, pt_low, A1, 0)
                at(s, par, 3, maxima, A1, 3)
                at(s, par, 1, pt_low, A0, 3)
                at(s, par, 0, stats, A0.norm)

            run(dve, step)

        @block.tensor
        def _(pe):
            t = nc.tensor

            pe.wait_ge(c_in, 32)
            pe.wait_ge(r_q, 3)
            for k in range(KC):
                for n in range(KC):
                    t.transpose(A0.X[:, k * D + n * P:k * D + (n + 1) * P], rhs_qT[:, n, k * P:(k + 1) * P], ident)
            for n in range(KC):
                i = t.matmul(A0.Y[:, n * P:(n + 1) * P], rhs_am[:, 2 + n:3 + n].to_broadcast([P, P]), ident,
                             start=True, stop=True)
            i.then_inc(r_t, 1)
            pe.wait_ge(r_q, 5)
            settled(pe)

            def norm_t(b, par, N):
                upto(pe, N.xn_ready, b)
                if N is FN:
                    before(pe, acc_ready, b, NE)
                elif N is A0.norm:
                    before(pe, A0.x_done, b)
                else:
                    before(pe, qt_done, b)
                for c in range(KC):
                    i = t.transpose(N.bank[:, c * S:(c + 1) * S], N.xn[:, c * P:(c + 1) * P], ident)
                i.then_inc(N.xt_ready, 1)

            def qk(b, par, A):
                at_first(pe, (w0_in, w1_in)[A.which], b)
                upto(pe, A.norm.xt_done, b)
                pe.wait_ge(A.ctx_in[par], dma_nth(b, par))
                if A.which == 1:
                    before(pe, qy_ready, b)
                for j, src in enumerate((A.norm.xt, A.ctx[par])):
                    for c in range(KC):
                        for k in range(KC):
                            i = t.matmul(A.X[:, j * D + c * S:j * D + (c + 1) * S],
                                         wslice(A.w + j * KC * D, k, c * P, P, D), src[:, k, :],
                                         start=(k == 0), stop=(k == KC - 1))
                i.then_inc(A.qk_ready, 1)

            def vproj(b, par, A):
                at_first(pe, (w0_in, w1_in)[A.which], b)
                pe.wait_ge(A.ctx_in[par], dma_nth(b, par))
                before(pe, A.ot_done, b)
                for k in range(KC):
                    i = t.matmul(A.Y[:, 0:D], A.ctx[par][:, k, :], wslice(A.w + 2 * KC * D, k, 0, D, D),
                                 start=(k == 0), stop=(k == KC - 1))
                i.then_inc(A.v_ready, 1)

            def scores(b, par, A, u):
                if u == 0:
                    upto(pe, A.k_done, b)
                if u == 1:
                    upto(pe, A.v_done, b)
                if u >= 2:
                    upto(pe, A.t_ready, b, NU, u - 1)
                for g in range(2):
                    r = 2 * HD * u
                    i = t.matmul(A.bank(u)[:, g * 2 * S:(g + 1) * 2 * S], A.q[r:r + 2 * HD, g, :],
                                 A.k[r:r + 2 * HD, g, :, :], start=True, stop=True)
                i.then_inc(A.s_ready, 1)

            def weights_t(b, par, A, u):
                upto(pe, A.p_ready, b, NU, u + 1)
                if u > 0:
                    upto(pe, A.pt_done, b, NU, u)
                for j in range(UH):
                    i = t.transpose(A.Z[:, j * S:(j + 1) * S], A.p[:, u, j, :], ident)
                i.then_inc(A.pt_ready, 1)

            def weighted(b, par, A, u):
                upto(pe, A.pt_done, b, NU, u + 1)
                if u == 0:
                    upto(pe, A.t_ready, b, NU)
                    upto(pe, A.v_low_done, b)
                for j in range(UH):
                    c, hh = j // 2, 2 * u + j % 2
                    bank, o, parts = (A.X, A.Y)[c], hh * VW, A.v_parts[:, c * HC + hh, :]
                    t.matmul(bank[:, o:o + VW], A.pt_high[:, u, j, :], parts, start=True, stop=False)
                    i = t.matmul(bank[:, o:o + VW - HD], A.pt_low[:, u, j, :], parts[:, 0:VW - HD], start=False,
                                 stop=True)
                i.then_inc(A.av_ready, 1)

            def out_t(b, par, A):
                upto(pe, A.o_ready, b)
                o = A.o[:, :, :].rearrange("p h d -> p (h d)")
                for c in range(KC):
                    i = t.transpose(A.Y[:, c * S:(c + 1) * S], o[:, c * P:(c + 1) * P], ident)
                i.then_inc(A.ot_ready, 1)

            def out_proj(b, par, A):
                upto(pe, A.ot_done, b)
                for k in range(KC):
                    i = t.matmul(A.Z[:, 0:D], A.ot[:, k, :], wslice(A.w + 3 * KC * D, k, 0, D, D),
                                 start=(k == 0), stop=(k == KC - 1))
                i.then_inc(A.y_ready, 1)

            def logits(b, par):
                upto(pe, FN.xt_done, b)
                for k in range(KC):
                    i = t.matmul(F1[:, 0:E], FN.xt[:, k, :], csl("rw", k * E, E), start=(k == 0), stop=(k == KC - 1))
                i.then_inc(lgm_ready, 1)

            def gates_t(b, par):
                upto(pe, cf_ready, b)
                t.transpose(F1[0:NE, 0:S], cf9[:, :], ident).then_inc(cft_ready, 1)

            def hidden(b, par, i):
                at_first(pe, wf_in, b)
                if i == 0:
                    upto(pe, FN.xt_done, b)
                if i == 1:
                    upto(pe, cft_done, b)
                if i == 2:
                    upto(pe, h_ready, b, len(HU), 1)
                lo, hi = HU[i]
                for e in range(lo, hi):
                    o = (F0, F1)[i % 2][:, (e - lo) * S:(e - lo + 1) * S]
                    off = 2 * ATT_W + e * KC * HID
                    for k in range(KC):
                        n = t.matmul(o, wslice(off, k, 0, HID, HID), FN.xt[:, k, :], start=(k == 0),
                                     stop=(k == KC - 1))
                n.then_inc(hm_ready, 1)

            def expert(bank, e, half_, first):
                return t.matmul(bank[:, half_ * D:(half_ + 1) * D], h[:, e, :],
                                wslice(2 * ATT_W + W1_W, e, 0, D, D), start=first, stop=True)

            def shared_out(b, par):
                at_first(pe, b2_in, b)
                upto(pe, h_ready, b, len(HU), 2)
                t.matmul(F1[:, 0:D], cfT[:, :], b2_sb[:, :], start=True, stop=False)
                expert(F1, 0, 0, False).then_inc(ym_ready, 1)

            def pair_out(b, par, j):
                if j == 0:
                    upto(pe, h_ready, b, len(HU))
                if j == 1:
                    upto(pe, acc_ready, b, NE, 1)
                if j >= 2:
                    upto(pe, acc_ready, b, NE, 2 * (j - 2) + 3)
                bank = (F0, F1)[j % 2]
                expert(bank, 1 + 2 * j, 0, True)
                expert(bank, 2 + 2 * j, 1, True).then_inc(ym_ready, 1)

            def q_t(b, par):
                upto(pe, qb_ready, b)
                for c in range(KC):
                    i = t.transpose(A1.Z[:, c * (S // 2):(c + 1) * (S // 2)].bitcast(BF16), qb[:, c * P:(c + 1) * P],
                                    ident_b[:, :])
                i.then_inc(qt_ready, 1)

            def q_mm(b, par):
                upto(pe, qt_done, b)
                for k in range(KC):
                    i = t.matmul(A1.X[:, 0:D], qT[:, k, :], rhs_q[:, k, :], start=(k == 0), stop=(k == KC - 1))
                i.then_inc(qm_ready, 1)

            def step(s, par):
                at(s, par, 2, out_t, A0)
                at(s, par, 4, weighted, A1, 1)
                at(s, par, 4, weighted, A1, 2)
                at(s, par, 3, pair_out, 2)
                at(s, par, 4, weighted, A1, 3)
                at(s, par, 2, out_proj, A0)
                at(s, par, 3, pair_out, 3)
                at(s, par, 4, out_t, A1)
                at(s, par, 1, norm_t, A0.norm)
                at(s, par, 4, out_proj, A1)
                at(s, par, 1, qk, A0)
                at(s, par, 2, norm_t, FN)
                at(s, par, 1, vproj, A0)
                at(s, par, 2, logits)
                at(s, par, 3, vproj, A1)
                at(s, par, 1, scores, A0, 0)
                at(s, par, 4, q_t)
                at(s, par, 1, scores, A0, 1)
                at(s, par, 4, q_mm)
                at(s, par, 3, norm_t, A1.norm)
                at(s, par, 1, scores, A0, 2)
                at(s, par, 3, qk, A1)
                at(s, par, 1, scores, A0, 3)
                at(s, par, 1, weights_t, A0, 0)
                at(s, par, 3, scores, A1, 0)
                at(s, par, 3, scores, A1, 1)
                at(s, par, 1, weights_t, A0, 1)
                at(s, par, 2, hidden, 0)
                at(s, par, 1, weights_t, A0, 2)
                at(s, par, 3, scores, A1, 2)
                at(s, par, 3, weights_t, A1, 0)
                at(s, par, 3, scores, A1, 3)
                at(s, par, 2, gates_t)
                at(s, par, 1, weighted, A0, 0)
                at(s, par, 1, weights_t, A0, 3)
                at(s, par, 2, hidden, 1)
                at(s, par, 1, weighted, A0, 1)
                at(s, par, 1, weighted, A0, 2)
                at(s, par, 3, weights_t, A1, 1)
                at(s, par, 2, hidden, 2)
                at(s, par, 1, weighted, A0, 3)
                at(s, par, 2, shared_out)
                at(s, par, 2, pair_out, 0)
                at(s, par, 3, weights_t, A1, 2)
                at(s, par, 2, pair_out, 1)
                at(s, par, 3, weights_t, A1, 3)
                at(s, par, 3, weighted, A1, 0)

            run(pe, step)


_INS = ("x", "ctxT", "mask", "weights", "cols", "rows", "b2", "rel", "rhsT")


def lay_out(i):
    import numpy as np

    def a(n):
        return np.ascontiguousarray(i[n])

    def chunks(w):
        return w.reshape(-1, P, w.shape[-1]).transpose(1, 0, 2).reshape(P, -1)

    att = [chunks(a(f"L{layer}_xattn_{n}").T) for layer, names in ((0, ("Wq", "Wk", "Wv", "Wo")),
                                                                  (1, ("w_q", "w_k", "w_v", "w_o"))) for n in names]
    w1 = [chunks(a("L0_ffn_sW1"))] + [chunks(w) for w in a("L0_ffn_rW1")]
    w2 = [a("L0_ffn_sW2")] + list(a("L0_ffn_rW2"))
    weights = np.concatenate(att + w1 + w2, axis=1)
    r = np.arange(P)
    f = np.float32
    q, key = r[:, None], r[None, :]
    inside = (key - q + W - 1 >= 0) & (key <= q) & (key - q + W - 1 <= q)
    pads = np.where(r < W - 1, np.minimum(r, W - 2 - r) + 1, 0)
    cols = np.concatenate([
        a("L0_xattn_bq").reshape(KC, P).T, a("L0_xattn_bk").reshape(KC, P).T,
        np.concatenate([a("L0_ffn_sb1")[None], a("L0_ffn_rb1")]).T,
        chunks(a("L0_ffn_routing_W").T),
        (r // HD % 2 == 0).astype(f)[:, None], (r // HD % 2 == 1).astype(f)[:, None],
        np.where(r < W - 1, 0.0, HUGE).astype(f)[:, None], (WSCALE * pads).astype(f)[:, None],
        np.eye(P, dtype=f), np.where(inside, 0.0, MASKED).astype(f), np.zeros((P, 6), f)], axis=1)
    rows = np.concatenate([a("L0_xattn_bv"), a("L0_xattn_bo"), a("L0_ffn_expert_bias"),
                           np.stack([a("g_xattn")[0], a("g_xattn")[1], a("g_ffn")[0], a("g_ffn")[1]])])
    b2 = np.concatenate([a("L0_ffn_rb2"), a("L0_ffn_sb2")[None]])
    ctxT = a("ctx_1024").reshape(B, S, KC, P).transpose(0, 3, 2, 1)
    at = r[:, None] - r[None, :] + a("L1_xattn_rel_emb").shape[0] // 2
    by_unit = np.arange(H).reshape(KC, NU, 2).transpose(1, 0, 2).reshape(-1)
    rel = a("L1_xattn_rel_emb")[at].transpose(0, 2, 1)[:, by_unit]
    rhsT = a("L1_ffn_rhs").T.reshape(KC, P, D).transpose(1, 0, 2)
    mask = a("mask_Bx1xSxS2_bf1").reshape(B, S, S).view(np.uint8)
    return {"x": a("x"), "ctxT": ctxT, "mask": mask, "weights": weights, "cols": cols, "rows": rows, "b2": b2,
            "rel": rel, "rhsT": rhsT}


def kernel(**inputs):
    import numpy as _np
    import concourse.bacc as _bacc
    from concourse import mybir as _mybir
    from concourse.bass_utils import run_bass_kernel_spmd as _run

    nc = _bacc.Bacc("TRN2", target_bir_lowering=False, num_devices=1)
    arrays, args = {}, []
    laid = lay_out(inputs)
    for name in _INS:
        v = _np.ascontiguousarray(laid[name])
        arrays[f"in_{name}_dram"] = v
        args.append(nc.dram_tensor(f"in_{name}_dram", v.shape, _mybir.dt.from_np(v.dtype), kind="ExternalInput").ap())
    args.append(nc.dram_tensor("out_0_dram", (B, S, D), _mybir.dt.float32, kind="ExternalOutput").ap())
    build(nc, *args)
    r = _run(nc, [arrays], core_ids=[0])
    return r.results[0]["out_0_dram"]
```
